# Optimizing a Trainium2 kernel written in Bass

```python
import numpy as np
import jax
import jax.numpy as jnp

def _softmax(x, axis=-1):
    return jax.nn.softmax(x, axis=axis)

def _gelu(x):
    return jax.nn.gelu(x, approximate=True)

def _silu(x):
    return jax.nn.silu(x)

def _sigmoid(x):
    return jax.nn.sigmoid(x)

def _layernorm(x, axis=-1, eps=1e-05):
    m = jnp.mean(x, axis=axis, keepdims=True)
    v = jnp.var(x, axis=axis, keepdims=True)
    return (x - m) / jnp.sqrt(v + eps)

def _scatter_add(tgt, idx, src, axis=0):
    return tgt.at[idx].add(src)

def _segment_sum(src, seg, n):
    return jax.ops.segment_sum(src, seg, n)
kernel_name = 'mk_cond_resid_d4_seqx_r4_b38c88'

def setup_inputs(seed: int=0):
    np.random.seed(seed)
    _w = jnp.asarray

    def _rec_inputs():
        import jax
        import jax.numpy as jnp
        _rk = jax.random.key(seed)
        x = 4.136e-05 + 0.9999 * jax.random.normal(jax.random.fold_in(_rk, 1), (128, 64, 256), jnp.float32)
        _lenS = 64 - jax.random.randint(jax.random.fold_in(_rk, 7), (128,), 0, max(1, 64 // 4) + 1, jnp.int32)
        _lenS2 = 64 - jax.random.randint(jax.random.fold_in(_rk, 8), (128,), 0, max(1, 64 // 4) + 1, jnp.int32)
        cond_1024 = -0.00608245 + 1.00131 * jax.random.normal(jax.random.fold_in(_rk, 11), (128, 256), jnp.float32)
        itok_BxS_2_50255 = jax.random.randint(jax.random.fold_in(_rk, 12), (128, 64), 2, 12564, jnp.int32)
        return (x, cond_1024, itok_BxS_2_50255)
    x, cond_1024, itok_BxS_2_50255 = _rec_inputs()

    def _L0_cond_setup():
        import jax, jax.numpy as jnp
        import numpy as np
        B, T, D_IN, V_IN, E = (64, 128, 256, 256, 256)
        key = jax.random.key(seed)
        ks = jax.random.split(key, 16)
        s = 0.01
        return {'video': jax.random.normal(ks[0], (B, V_IN), jnp.float32), 'seq': jax.random.normal(ks[1], (B, T, D_IN), jnp.float32), 'W_z': jax.random.normal(ks[2], (D_IN, E), jnp.float32) * s, 'U_z': jax.random.normal(ks[3], (E, E), jnp.float32) * s, 'C_z': jax.random.normal(ks[4], (V_IN, E), jnp.float32) * s, 'b_z': jnp.zeros((E,), jnp.float32), 'W_r': jax.random.normal(ks[5], (D_IN, E), jnp.float32) * s, 'U_r': jax.random.normal(ks[6], (E, E), jnp.float32) * s, 'C_r': jax.random.normal(ks[7], (V_IN, E), jnp.float32) * s, 'b_r': jnp.zeros((E,), jnp.float32), 'W': jax.random.normal(ks[8], (D_IN, E), jnp.float32) * s, 'U': jax.random.normal(ks[9], (E, E), jnp.float32) * s, 'C': jax.random.normal(ks[10], (V_IN, E), jnp.float32) * s, 'b': jnp.zeros((E,), jnp.float32)}
    _L0_cond_all = _L0_cond_setup()
    _L0_cond_in = {k: v for k, v in _L0_cond_all.items() if k in ('W_z', 'U_z', 'C_z', 'b_z', 'W_r', 'U_r', 'C_r', 'b_r', 'W', 'U', 'C', 'b')}
    del _L0_cond_all

    def _L1_cond_setup():
        import jax, jax.numpy as jnp
        import numpy as np
        HASH_PRIME = 5099
        MIN_CAPACITY = 4
        key = jax.random.key(seed)
        ks = jax.random.split(key, 8)
        B, T, D, F, E = (8, 512, 256, 512, 16)
        return {'x': jax.random.normal(ks[0], (B, T, D), dtype=jnp.float32), 'token_ids': jax.random.randint(ks[1], (B, T), 0, 50257, dtype=jnp.int32), 'shift_state': jax.random.normal(ks[2], (B, D), dtype=jnp.float32), 'time_maa_k': jax.random.uniform(ks[3], (D,), dtype=jnp.float32), 'time_maa_r': jax.random.uniform(ks[4], (D,), dtype=jnp.float32), 'w_recept': jax.random.normal(ks[5], (D, D), dtype=jnp.float32) * 0.02, 'w_key': jax.random.normal(ks[6], (E, D, F), dtype=jnp.float32) * 0.02, 'w_value': jax.random.normal(ks[7], (E, F, D), dtype=jnp.float32) * 0.02}
    _L1_cond_all = _L1_cond_setup()
    _L1_cond_in = {k: v for k, v in _L1_cond_all.items() if k in ('time_maa_k', 'time_maa_r', 'w_recept', 'w_key', 'w_value')}
    del _L1_cond_all

    def _L2_cond_setup():
        import jax, jax.numpy as jnp
        import numpy as np
        LATENT = 256
        key = jax.random.key(seed)
        k1, k2, k3, k4 = jax.random.split(key, 4)
        B, T, D = (64, 128, LATENT)
        h_t = jax.random.normal(k1, (B, D), dtype=jnp.float32)
        z = jax.random.normal(k2, (B, T, D), dtype=jnp.float32)
        bound = 1.0 / np.sqrt(2 * D)
        W = jax.random.uniform(k3, (D, 2 * D), minval=-bound, maxval=bound, dtype=jnp.float32)
        b = jax.random.uniform(k4, (D,), minval=-bound, maxval=bound, dtype=jnp.float32)
        alpha = jnp.full((D,), 0.1, dtype=jnp.float32)
        return {'h_t': h_t, 'z': z, 'W': W, 'b': b, 'alpha': alpha}
    _L2_cond_all = _L2_cond_setup()
    _L2_cond_in = {k: v for k, v in _L2_cond_all.items() if k in ('W', 'b', 'alpha')}
    del _L2_cond_all

    def _L3_cond_setup():
        import jax, jax.numpy as jnp
        import numpy as np
        import math
        N, T, D, H = (128, 128, 256, 256)
        key = jax.random.key(seed)
        k1, k2, k3, k4 = jax.random.split(key, 4)
        x = jax.random.normal(k1, (N, T, D), dtype=jnp.float32)
        h0 = jax.random.normal(k2, (N, H), dtype=jnp.float32)
        Wx = jax.random.normal(k3, (D, H), dtype=jnp.float32) / math.sqrt(D)
        Wh = jax.random.normal(k4, (H, H), dtype=jnp.float32) / math.sqrt(H)
        b = jnp.zeros((H,), dtype=jnp.float32)
        return {'x': x, 'h0': h0, 'Wx': Wx, 'Wh': Wh, 'b': b}
    _L3_cond_all = _L3_cond_setup()
    _L3_cond_in = {k: v for k, v in _L3_cond_all.items() if k in ('Wx', 'Wh', 'b')}
    del _L3_cond_all
    return {'x': x, 'cond_1024': cond_1024, 'itok_BxS_2_50255': itok_BxS_2_50255, 'L0_cond_W_z': _L0_cond_in['W_z'], 'L0_cond_U_z': _L0_cond_in['U_z'], 'L0_cond_C_z': _L0_cond_in['C_z'], 'L0_cond_b_z': _L0_cond_in['b_z'], 'L0_cond_W_r': _L0_cond_in['W_r'], 'L0_cond_U_r': _L0_cond_in['U_r'], 'L0_cond_C_r': _L0_cond_in['C_r'], 'L0_cond_b_r': _L0_cond_in['b_r'], 'L0_cond_W': _L0_cond_in['W'], 'L0_cond_U': _L0_cond_in['U'], 'L0_cond_C': _L0_cond_in['C'], 'L0_cond_b': _L0_cond_in['b'], 'L1_cond_time_maa_k': _L1_cond_in['time_maa_k'], 'L1_cond_time_maa_r': _L1_cond_in['time_maa_r'], 'L1_cond_w_recept': _L1_cond_in['w_recept'], 'L1_cond_w_key': _L1_cond_in['w_key'], 'L1_cond_w_value': _L1_cond_in['w_value'], 'L2_cond_W': _L2_cond_in['W'], 'L2_cond_b': _L2_cond_in['b'], 'L2_cond_alpha': _L2_cond_in['alpha'], 'L3_cond_Wx': _L3_cond_in['Wx'], 'L3_cond_Wh': _L3_cond_in['Wh'], 'L3_cond_b': _L3_cond_in['b']}

def reference(x, cond_1024, itok_BxS_2_50255, L0_cond_W_z, L0_cond_U_z, L0_cond_C_z, L0_cond_b_z, L0_cond_W_r, L0_cond_U_r, L0_cond_C_r, L0_cond_b_r, L0_cond_W, L0_cond_U, L0_cond_C, L0_cond_b, L1_cond_time_maa_k, L1_cond_time_maa_r, L1_cond_w_recept, L1_cond_w_key, L1_cond_w_value, L2_cond_W, L2_cond_b, L2_cond_alpha, L3_cond_Wx, L3_cond_Wh, L3_cond_b):
    import jax
    import jax.numpy as jnp

    def _L0_cond_ref(video, seq, W_z, U_z, C_z, b_z, W_r, U_r, C_r, b_r, W, U, C, b):
        import jax, jax.numpy as jnp
        import numpy as np
        B, T, D_IN, V_IN, E = (64, 128, 256, 256, 256)
        vz = video @ C_z + b_z
        vr = video @ C_r + b_r
        vh = video @ C + b
        xz = jnp.einsum('btd,de->bte', seq, W_z)
        xr = jnp.einsum('btd,de->bte', seq, W_r)
        xh = jnp.einsum('btd,de->bte', seq, W)

        def step(h, xs):
            xzt, xrt, xht = xs
            z = jax.nn.sigmoid(xzt + h @ U_z + vz)
            r = jax.nn.sigmoid(xrt + h @ U_r + vr)
            hh = jnp.tanh(xht + r * h @ U + vh)
            h_new = (1.0 - z) * h + z * hh
            return (h_new, h_new)
        h0 = jnp.zeros((seq.shape[0], U.shape[0]), seq.dtype)
        xs = (jnp.swapaxes(xz, 0, 1), jnp.swapaxes(xr, 0, 1), jnp.swapaxes(xh, 0, 1))
        _, out_t = jax.lax.scan(step, h0, xs)
        return jnp.swapaxes(out_t, 0, 1)

    def _L1_cond_ref(x, token_ids, shift_state, time_maa_k, time_maa_r, w_recept, w_key, w_value):
        import jax, jax.numpy as jnp
        import numpy as np
        HASH_PRIME = 5099
        MIN_CAPACITY = 4
        B, T, D = x.shape
        E = w_key.shape[0]
        N = B * T
        C = max(MIN_CAPACITY, N // E)
        xprev = jnp.concatenate([shift_state[:, None, :], x[:, :-1]], axis=1)
        dxprev = xprev - x
        xk = x + dxprev * time_maa_k
        xr = x + dxprev * time_maa_r
        e_idx = token_ids.reshape(N).astype(jnp.int32) * HASH_PRIME % E
        onehot = (e_idx[:, None] == jnp.arange(E, dtype=jnp.int32)[None, :]).astype(jnp.int32)
        pos = jnp.take_along_axis(jnp.cumsum(onehot, axis=0), e_idx[:, None], axis=1)[:, 0] - 1
        keep = pos < C
        slot = jnp.where(keep, e_idx * C + pos, E * C)
        xk_flat = xk.reshape(N, D)
        buf = jnp.zeros((E * C + 1, D), dtype=x.dtype).at[slot].set(xk_flat)
        expert_in = buf[:E * C].reshape(E, C, D)
        h = jnp.square(jax.nn.relu(jnp.einsum('ecd,edf->ecf', expert_in, w_key)))
        expert_out = jnp.einsum('ecf,efd->ecd', h, w_value)
        out_pad = jnp.concatenate([expert_out.reshape(E * C, D), jnp.zeros((1, D), dtype=x.dtype)], axis=0)
        y = out_pad[slot].reshape(B, T, D)
        r = jax.nn.sigmoid(jnp.einsum('btd,ed->bte', xr, w_recept))
        return r * y

    def _L2_cond_ref(h_t, z, W, b, alpha):
        import jax, jax.numpy as jnp
        import numpy as np
        LATENT = 256
        D = h_t.shape[-1]
        Wh = W[:, :D]
        Wz = W[:, D:]
        leak = 1.0 - alpha

        def step(h, z_t):
            gate = jax.nn.sigmoid(h @ Wh.T + z_t @ Wz.T + b)
            h_new = jnp.tanh(h * leak + gate * z_t)
            return (h_new, h_new)
        _, hs = jax.lax.scan(step, h_t, jnp.swapaxes(z, 0, 1))
        return jnp.swapaxes(hs, 0, 1)

    def _L3_cond_ref(x, h0, Wx, Wh, b):
        import jax, jax.numpy as jnp
        import numpy as np
        import math
        N, T, D, H = (128, 128, 256, 256)
        xW = jnp.einsum('ntd,dh->nth', x, Wx) + b

        def step(h_prev, xw_t):
            h_next = jnp.tanh(h_prev @ Wh + xw_t)
            return (h_next, h_next)
        _, hs = jax.lax.scan(step, h0, jnp.swapaxes(xW, 0, 1))
        return jnp.swapaxes(hs, 0, 1)
    x = x + _L0_cond_ref(cond_1024, x, L0_cond_W_z, L0_cond_U_z, L0_cond_C_z, L0_cond_b_z, L0_cond_W_r, L0_cond_U_r, L0_cond_C_r, L0_cond_b_r, L0_cond_W, L0_cond_U, L0_cond_C, L0_cond_b)
    x = x + _L1_cond_ref(x, itok_BxS_2_50255, cond_1024, L1_cond_time_maa_k, L1_cond_time_maa_r, L1_cond_w_recept, L1_cond_w_key, L1_cond_w_value)
    x = x + _L2_cond_ref(cond_1024, x, L2_cond_W, L2_cond_b, L2_cond_alpha)
    x = x + _L3_cond_ref(x, cond_1024, L3_cond_Wx, L3_cond_Wh, L3_cond_b)
    return x

_drawn_inputs = setup_inputs


def setup_inputs(seed=0):
    import zlib

    import numpy as np

    out = dict(_drawn_inputs(seed))
    spreads = {'L0_cond_b_z': (0.0, 0.8),
     'L0_cond_b_r': (0.0, 2.0),
     'L0_cond_b': (0.0, 0.1),
     'L2_cond_alpha': (0.10000000149011612, 0.6),
     'L3_cond_b': (0.0, 2.0)}
    factors = {'L0_cond_W_z': 5.86,
     'L0_cond_U_z': 32.864,
     'L0_cond_C_z': 8.0,
     'L0_cond_W_r': 64.0,
     'L0_cond_U_r': 64.0,
     'L0_cond_C_r': 64.0,
     'L1_cond_time_maa_k': 5.515,
     'L1_cond_time_maa_r': 8.0,
     'L1_cond_w_recept': 8.0,
     'L1_cond_w_key': 3.051,
     'L1_cond_w_value': 2.776,
     'L2_cond_b': 200.0,
     'L0_cond_U': 5.153,
     'L3_cond_Wh': 4.893}
    for name, (base, spread) in spreads.items():
        noise = np.random.default_rng([zlib.crc32(name.encode()), seed]).standard_normal(out[name].shape)
        drawn = base * np.exp(spread * noise) if base else spread * noise
        out[name] = jnp.asarray(drawn.astype(out[name].dtype))
    for name, factor in factors.items():
        out[name] = (out[name] * factor).astype(out[name].dtype)
    return out
```

```python
import numpy as np
from contextlib import ExitStack

import concourse.bass as bass
import concourse.mybir as mybir

F32 = mybir.dt.float32
I32 = mybir.dt.int32
U32 = mybir.dt.uint32
ALU = mybir.AluOpType
ACT = mybir.ActivationFunctionType
AX = mybir.AxisListType

P = 128
B, T, D = 128, 64, 256
K = D // P
W = K * B
E, F = 16, 512
C = B * T // E
FT = F // P
ST = C // P
NSLOT = E * C
HASH = 5099 % E
NVEC = 8
V_BZ, V_BR, V_BH, V_MK, V_MR, V_B2, V_AL, V_B3 = range(NVEC)
(W_Z, W_R, W_H, U_Z, U_R, U_H, C_Z, C_R, C_H, W_REC, L2_H, L2_Z, L3_X, L3_H) = range(14)
NW = 14


def build(nc, x, cond, ids, mats, vecs, w_key, w_value, out, rows, yrows):
    with ExitStack() as ctx:
        def sb(name, shape, dt=F32):
            return ctx.enter_context(nc.sbuf_tensor(name, shape, dt))

        def sem(name):
            return ctx.enter_context(nc.semaphore(name))

        bank = [ctx.enter_context(nc.psum_tensor(f"bank{i}", [P, 512], F32)) for i in range(8)]

        xs = sb("xs", [P, (T + 1) * W])
        rr = sb("rr", [P, T * W])
        wm = sb("wm", [P, NW, K, D])
        vec = sb("vec", [P, NVEC, K])
        ident = sb("ident", [P, P])
        vr, vz, vc = (sb(n, [P, W]) for n in ("vr", "vz", "vc"))
        leak_t, b2_t = sb("leak_t", [P, W]), sb("b2_t", [P, W])
        leak = sb("leak", [P, K])
        h = sb("h", [P, 2, W])
        rg, zg, hh = sb("rg", [P, W]), sb("zg", [P, W]), sb("hh", [P, W])
        rh, wh, ph = sb("rh", [P, W]), sb("wh", [P, W]), sb("ph", [P, W])
        dx = sb("dx", [P, 2, W])
        mixed = sb("mixed", [P, 2, W])
        xk, xr = mixed[:, 0, :], mixed[:, 1, :]
        row = sb("row", [P, 2, D])
        slot_i = sb("slot_i", [P, T], I32)
        idx = sb("idx", [P, 2], I32)
        wk = sb("wk", [P, 2, K, F])
        wv = sb("wv", [P, 2, FT, D])
        ein = sb("ein", [P, 2, ST, D])
        einT = sb("einT", [P, K, C])
        hid = wm[:, 0:4, :, :].rearrange("p m k d -> p (m k d)").rearrange("p (f c) -> p f c", f=FT)
        yo = wm[:, 4:8, :, :].rearrange("p m k d -> p (m k d)").rearrange("p (u s d) -> p u s d", u=2, s=ST)
        hrel = wm[:, 8:10, :, :].rearrange("p m k d -> p (m k d)").rearrange("p (u c) -> p u c", u=2)

        ET = E * T
        onehot = rr[:, 0:ET].rearrange("p (e t) -> p e t", t=T)
        onehot_f = rr[:, 0:ET]
        eidx = rr[:, ET:2 * ET].rearrange("p (e t) -> p e t", t=T)
        carry = rr[:, 2 * ET:3 * ET]
        count = rr[:, 3 * ET:4 * ET]
        count3 = count.rearrange("p (e t) -> p e t", t=T)
        total = rr[:, 4 * ET:4 * ET + E]
        before = rr[:, 4 * ET + E:4 * ET + 2 * E]
        lower = rr[:, 4 * ET + 64:4 * ET + 64 + P]
        ef = rr[:, 5 * ET:5 * ET + T]
        pos = rr[:, 5 * ET + T:5 * ET + 2 * T]
        keep = rr[:, 5 * ET + 2 * T:5 * ET + 3 * T]
        slot_f = rr[:, 5 * ET + 3 * T:5 * ET + 4 * T]
        id_i = sb("id_i", [P, T], I32)
        zeros = sb("zeros", [P, W])

        x_in = sem("x_in")
        w_in = sem("w_in")
        c_in = sem("c_in")
        id_in = sem("id_in")
        zfill = sem("zfill")
        zeros_set = sem("zeros_set")
        consts = sem("consts")
        const_step = sem("const_step")
        route_step = sem("route_step")
        total_ready = sem("total_ready")
        before_mm = sem("before_mm")
        slots_ready = sem("slots_ready")
        v_mm = sem("v_mm")
        v_ready = sem("v_ready")
        h_ready = sem("h_ready")
        r_proj, z_proj, c_proj = sem("r_proj"), sem("z_proj"), sem("c_proj")
        rv_ready, zv_ready, cv_ready = sem("rv_ready"), sem("zv_ready"), sem("cv_ready")
        r_mm, z_mm, c_mm = sem("r_mm"), sem("z_mm"), sem("c_mm")
        r_sig, z_sig, c_tanh = sem("r_sig"), sem("z_sig"), sem("c_tanh")
        rh_ready, wh_ready, ph_ready = sem("rh_ready"), sem("wh_ready"), sem("ph_ready")
        x1_ready, dx_ready = sem("x1_ready"), sem("dx_ready")
        xk_ready, xr_ready = sem("xk_ready"), sem("xr_ready")
        rec_mm, rec_sig = sem("rec_mm"), sem("rec_sig")
        tr_mm, row_ready = sem("tr_mm"), sem("row_ready")
        idx_ready = sem("idx_ready")
        scat = [sem("scat0"), sem("scat1")]
        ex_in = [sem("ex_in0"), sem("ex_in1")]
        einT_mm, einT_ready = sem("einT_mm"), sem("einT_ready")
        h_mm, rel_ready, hid_ready = sem("h_mm"), sem("rel_ready"), sem("hid_ready")
        o_mm, o_ready = sem("o_mm"), sem("o_ready")
        y_out = [sem("y_out0"), sem("y_out1")]
        idy_ready = sem("idy_ready")
        gath = [sem("gath0"), sem("gath1")]
        yT_mm, ry_ready, x2_ready = sem("yT_mm"), sem("ry_ready"), sem("x2_ready")
        h2_ready, h3_ready = sem("h2_ready"), sem("h3_ready")
        hl_ready = sem("hl_ready")
        g_proj, gb_ready, g_mm, g_sig = sem("g_proj"), sem("gb_ready"), sem("g_mm"), sem("g_sig")
        gz_ready, pre_ready = sem("gz_ready"), sem("pre_ready")
        x3_ready, p3_mm, out_ready = sem("x3_ready"), sem("p3_mm"), sem("out_ready")
        stored = sem("stored")
        pool_paced = sem("pool_paced")

        h2, h3 = h, mixed
        g2 = rg
        gz, pre, hl = rh, ph, wh

        ZROWS = 512
        N_ZFILL = NSLOT // ZROWS

        def at(t, k=None):
            return bass.ds(t * W, W) if k is None else bass.ds(t * W + k * B, B)

        def half(k):
            return slice(k * B, (k + 1) * B)

        block = ctx.enter_context(nc.Block())

        @block.sync
        def _(sp):
            sp.dma_start(id_i[:, :], ids).then_inc(id_in, 16)
            sp.dma_start(xs[:, 0:W], cond).then_inc(c_in, 16)
            sp.dma_start(vec[:, :, :], vecs).then_inc(c_in, 16)
            sp.dma_start(xs[:, W:3 * W], x[:, 0:2 * W]).then_inc(x_in, 16)
            with sp.Fori(1, T // 2) as n:
                sp.wait_ge(x_in, n * 16)
                sp.dma_start(xs[:, bass.ds((2 * n + 1) * W, 2 * W)], x[:, bass.ds(n * 2 * W, 2 * W)]).then_inc(x_in, 16)
            sp.wait_ge(scat[0], 16 * (T // 2))
            sp.wait_ge(scat[1], 16 * (T // 2))

            def load(e, u):
                sp.dma_start(ein[:, u, :, :],
                             rows[bass.ds(e * C, C), :].rearrange("(s p) d -> p s d", p=P)).then_inc(ex_in[u], 16)
                sp.dma_start(wk[:, u, :, :], w_key[:, bass.ds(e * K * F, K * F)]
                             .rearrange("p (k f) -> p k f", k=K)).then_inc(ex_in[u], 16)
                sp.dma_start(wv[:, u, :, :], w_value[:, bass.ds(e * FT * D, FT * D)]
                             .rearrange("p (f d) -> p f d", f=FT)).then_inc(ex_in[u], 16)

            def store(e, u):
                sp.wait_ge(o_ready, (e + 1) * ST)
                sp.dma_start(yrows[bass.ds(e * C, C), :].rearrange("(s p) d -> p s d", p=P),
                             yo[:, u, :, :]).then_inc(y_out[u], 16)

            for e in range(2):
                load(e, e)
            with sp.Fori(1, E // 2) as n:
                for u in range(2):
                    sp.wait_ge(o_mm, (2 * n + u - 1) * ST)
                    load(2 * n + u, u)
                    store(2 * n + u - 2, u)
            for e in range(E - 2, E):
                store(e, e % 2)
            with sp.Fori(0, T // 2) as n:
                sp.wait_ge(out_ready, 2 * n + 2)
                sp.dma_start(out[:, bass.ds(n * 2 * W, 2 * W)], xs[:, bass.ds((2 * n + 1) * W, 2 * W)]).then_inc(stored, 16)
            sp.wait_ge(stored, 16 * (T // 2))

        @block.tensor
        def _(pe):
            R, Z, H = bank[0:2], bank[2:4], bank[4:6]
            REC, TR = bank[6], bank[7]

            def prod(dst, m, rhs, start, stop):
                for o in range(K):
                    for k in range(K):
                        mm = pe.matmul(dst[:, half(o)], wm[:, m, k, o * P:(o + 1) * P], rhs(k),
                                       start=start and o == 0 and k == 0,
                                       stop=stop and k == K - 1, skip_group_check=True)
                return mm

            pe.wait_ge(c_in, 32)
            pe.wait_ge(w_in, 16)
            for i, (m, dst) in enumerate(((C_R, R[0]), (C_Z, Z[0]), (C_H, H[0]))):
                prod(dst, m, lambda k: xs[:, half(k)], True, True).then_inc(v_mm, 1)
            pe.wait_ge(total_ready, 1)
            pe.matmul(REC[:, 0:E], lower, total, start=True, stop=True).then_inc(before_mm, 1)

            def x_at(t):
                return lambda k: xs[:, at(t + 1, k)]

            def receptance(t, first=False):
                pe.wait_ge(xr_ready, t + 1)
                if not first:
                    pe.wait_ge(rec_sig, t)
                prod(REC, W_REC, lambda k: xr[:, half(k)], True, True).then_inc(rec_mm, 1)

            def turn_rows(t, first=False):
                pe.wait_ge(xk_ready, t + 1)
                if not first:
                    pe.wait_ge(row_ready, t)
                for k in range(K):
                    mm = pe.transpose(TR[:, k * P:(k + 1) * P], xk[:, half(k)], ident[:, :])
                mm.then_inc(tr_mm, 1)

            def step(t, u, first=False, last=False):
                hp = lambda k: h[:, u, half(k)]
                pe.wait_ge(h_ready, t + 1)
                pe.wait_ge(rv_ready, t + 1)
                prod(R[u], U_R, hp, False, True).then_inc(r_mm, 1)
                pe.wait_ge(zv_ready, t + 1)
                prod(Z[u], U_Z, hp, False, True).then_inc(z_mm, 1)
                if not last:
                    pe.wait_ge(x_in, (t + 2 + u) * 8)
                    prod(R[1 - u], W_R, x_at(t + 1), True, False).then_inc(r_proj, 1)
                pe.wait_ge(cv_ready, t + 1)
                pe.wait_ge(rh_ready, t + 1)
                prod(H[u], U_H, lambda k: rh[:, half(k)], False, True).then_inc(c_mm, 1)
                if not last:
                    prod(Z[1 - u], W_Z, x_at(t + 1), True, False).then_inc(z_proj, 1)
                    prod(H[1 - u], W_H, x_at(t + 1), True, False).then_inc(c_proj, 1)
                if not first:
                    receptance(t - 1, first=isinstance(t, int) and t == 1)
                    turn_rows(t - 1, first=isinstance(t, int) and t == 1)

            pe.wait_ge(x_in, 16)
            pe.wait_ge(v_ready, 3)
            prod(R[0], W_R, x_at(0), True, False).then_inc(r_proj, 1)
            prod(Z[0], W_Z, x_at(0), True, False).then_inc(z_proj, 1)
            prod(H[0], W_H, x_at(0), True, False).then_inc(c_proj, 1)
            step(0, 0, first=True)
            step(1, 1)
            with pe.Fori(1, T // 2 - 1) as n:
                step(2 * n, 0)
                step(2 * n + 1, 1)
            step(T - 2, 0)
            step(T - 1, 1, last=True)
            receptance(T - 1)
            turn_rows(T - 1)

            TT, HB, OB = bank[0:2], bank[2:4], bank[4:6]

            def turn_in(e, u, n, first=False):
                pe.wait_ge(ex_in[u], (n + 1) * 48)
                if not first:
                    pe.wait_ge(einT_ready, e * K)
                for k in range(K):
                    for s in range(ST):
                        mm = pe.transpose(TT[k][:, s * P:(s + 1) * P], ein[:, u, s, k * P:(k + 1) * P], ident[:, :])
                    mm.then_inc(einT_mm, 1)

            def hidden(e, u, first=False):
                pe.wait_ge(einT_ready, (e + 1) * K)
                for f in range(FT):
                    if not (first and f < 2):
                        pe.wait_ge(rel_ready, e * FT + f - 1)
                    for k in range(K):
                        mm = pe.matmul(HB[f % 2][:, :], wk[:, u, k, f * P:(f + 1) * P], einT[:, k, :],
                                       start=k == 0, stop=k == K - 1)
                    mm.then_inc(h_mm, 1)

            def project(e, u, first=False):
                pe.wait_ge(hid_ready, (e + 1) * FT)
                for s in range(ST):
                    if not (first and s < 2):
                        pe.wait_ge(o_ready, e * ST + s - 1)
                    for f in range(FT):
                        mm = pe.matmul(OB[s % 2][:, 0:D], hid[:, f, s * P:(s + 1) * P], wv[:, u, f, :],
                                       start=f == 0, stop=f == FT - 1)
                    mm.then_inc(o_mm, 1)

            turn_in(0, 0, 0, first=True)
            hidden(0, 0, first=True)
            turn_in(1, 1, 0)
            project(0, 0, first=True)
            hidden(1, 1)
            turn_in(2, 0, 1)
            project(1, 1)
            with pe.Fori(1, E // 2 - 1) as n:
                hidden(2 * n, 0)
                turn_in(2 * n + 1, 1, n)
                project(2 * n, 0)
                hidden(2 * n + 1, 1)
                turn_in(2 * n + 2, 0, n + 1)
                project(2 * n + 1, 1)
            hidden(E - 2, 0)
            turn_in(E - 1, 1, E // 2 - 1)
            project(E - 2, 0)
            hidden(E - 1, 1)
            project(E - 1, 1)

            G, Q, Y = bank[0:2], bank[2:4], bank[6:8]

            def turn_y(t, u, m, first=False):
                pe.wait_ge(gath[u], (m + 1) * 16)
                if not first:
                    pe.wait_ge(ry_ready, t - 1)
                for k in range(K):
                    mm = pe.transpose(Y[u][:, k * B:(k + 1) * B], row[:, u, k * P:(k + 1) * P], ident[:, :])
                mm.then_inc(yT_mm, 1)

            def proj2(t, u):
                pe.wait_ge(x2_ready, t + 1)
                prod(G[u], L2_Z, x_at(t), True, False).then_inc(g_proj, 1)

            def l3(t, u, first=False):
                pe.wait_ge(x3_ready, t + 1)
                prod(Q[u], L3_X, x_at(t), True, False)
                pe.wait_ge(h3_ready, t + 1)
                prod(Q[u], L3_H, lambda k: h3[:, u, half(k)], False, True).then_inc(p3_mm, 1)

            def cstep(t, u, m, first=False, n_left=None):
                pe.wait_ge(h2_ready, t + 1)
                pe.wait_ge(gb_ready, t + 1)
                prod(G[u], L2_H, lambda k: h2[:, u, half(k)], False, True).then_inc(g_mm, 1)
                if n_left is None or n_left > 1:
                    proj2(t + 1, 1 - u)
                if not first:
                    l3(t - 1, 1 - u)
                if n_left is None or n_left > 3:
                    turn_y(t + 3, 1 - u, m)

            turn_y(0, 0, 0, first=True)
            turn_y(1, 1, 0, first=True)
            turn_y(2, 0, 1)
            proj2(0, 0)
            cstep(0, 0, 1, first=True)
            cstep(1, 1, 2)
            with pe.Fori(1, T // 2 - 2) as n:
                cstep(2 * n, 0, n + 1)
                cstep(2 * n + 1, 1, n + 2)
            for t in range(T - 4, T):
                cstep(t, t % 2, (t + 3) // 2, n_left=T - t)
            l3(T - 1, 1)

        @block.scalar
        def _(act):
            act.dma_start(wm[:, :, :, :], mats).then_inc(w_in, 16)
            R, Z, H = bank[0:2], bank[2:4], bank[4:6]
            REC, TR = bank[6], bank[7]

            def tail(t, u, n, first=False):
                act.wait_ge(rec_mm, t + 1)
                act.activation(rr[:, at(t)], REC[:, 0:W], ACT.Sigmoid).then_inc(rec_sig, 1)
                act.wait_ge(tr_mm, t + 1)
                if not first:
                    act.wait_ge(scat[u], n * 16)
                act.activation(row[:, u, :], TR[:, 0:D], ACT.Copy).then_inc(row_ready, 1)

            def gates(t, u):
                act.wait_ge(r_mm, t + 1)
                act.activation(rg[:, :], R[u][:, 0:W], ACT.Sigmoid).then_inc(r_sig, 1)
                act.wait_ge(z_mm, t + 1)
                act.activation(zg[:, :], Z[u][:, 0:W], ACT.Sigmoid).then_inc(z_sig, 1)
                act.wait_ge(c_mm, t + 1)
                act.activation(hh[:, :], H[u][:, 0:W], ACT.Tanh).then_inc(c_tanh, 1)

            act.wait_ge(slots_ready, 1)
            gates(0, 0)
            gates(1, 1)
            tail(0, 0, 0, first=True)
            gates(2, 0)
            tail(1, 1, 0, first=True)
            gates(3, 1)
            tail(2, 0, 1)
            with act.Fori(2, T // 2) as n:
                gates(2 * n, 0)
                tail(2 * n - 1, 1, n - 1)
                gates(2 * n + 1, 1)
                tail(2 * n, 0, n)
            tail(T - 1, 1, T // 2 - 1)

            HB, OB = bank[2:4], bank[4:6]

            def expert(e, u, n, first=False):
                for f in range(FT):
                    act.wait_ge(h_mm, e * FT + f + 1)
                    if not (first and f < 2):
                        act.wait_ge(hid_ready, e * FT + f - 1)
                    act.activation(hrel[:, f % 2, :], HB[f % 2][:, :], ACT.Relu).then_inc(rel_ready, 1)
                for s in range(ST):
                    act.wait_ge(o_mm, e * ST + s + 1)
                    if s == 0 and n is not None:
                        act.wait_ge(y_out[u], n * 16)
                    act.activation(yo[:, u, s, :], OB[s % 2][:, 0:D], ACT.Copy).then_inc(o_ready, 1)

            expert(0, 0, None, first=True)
            expert(1, 1, None)
            with act.Fori(1, E // 2) as n:
                expert(2 * n, 0, n)
                expert(2 * n + 1, 1, n)

            G, Q = bank[0:2], bank[2:4]

            def l2(t, u):
                act.wait_ge(g_mm, t + 1)
                act.activation(g2[:, :], G[u][:, 0:W], ACT.Sigmoid).then_inc(g_sig, 1)
                act.wait_ge(pre_ready, t + 1)
                act.activation(h2[:, 1 - u, :], pre[:, :], ACT.Tanh).then_inc(h2_ready, 1)

            def l3(t, u, first=False):
                act.wait_ge(p3_mm, t + 1)
                if not first:
                    act.wait_ge(out_ready, t - 1)
                for k in range(K):
                    a = act.activation(h3[:, 1 - u, half(k)], Q[u][:, half(k)], ACT.Tanh,
                                       bias=vec[:, V_B3, k:k + 1])
                a.then_inc(h3_ready, 1)

            l2(0, 0)
            l2(1, 1)
            l3(0, 0, first=True)
            l2(2, 0)
            l3(1, 1, first=True)
            l2(3, 1)
            l3(2, 0)
            with act.Fori(2, T // 2) as n:
                l2(2 * n, 0)
                l3(2 * n - 1, 1)
                l2(2 * n + 1, 1)
                l3(2 * n, 0)
            l3(T - 1, 1)

        @block.vector
        def _(dve):
            R, Z, H = bank[0:2], bank[2:4], bank[4:6]
            REC = bank[6]
            dve.memset(zeros[:, :], 0.0).then_inc(zeros_set, 1)
            dve.memset(h[:, 0, :], 0.0).then_inc(h_ready, 1)

            chain = [0]

            def link(ins):
                chain[0] += 1
                ins.then_inc(route_step, 1)
                dve.wait_ge(route_step, chain[0])

            dve.wait_ge(id_in, 16)
            link(dve.tensor_single_scalar(id_i[:, :], id_i[:, :], E - 1, ALU.bitwise_and))
            link(dve.tensor_single_scalar(id_i[:, :], id_i[:, :], float(HASH), ALU.mult))
            link(dve.tensor_single_scalar(id_i[:, :], id_i[:, :], E - 1, ALU.bitwise_and))
            link(dve.tensor_copy(ef, id_i[:, :]))
            dve.wait_ge(consts, 3)
            link(dve.tensor_tensor(onehot, eidx, ef.unsqueeze(1).broadcast_to([P, E, T]), ALU.is_equal))
            link(dve.tensor_tensor_scan(count, carry, onehot_f, 0.0, ALU.mult, ALU.add))
            dve.tensor_copy(total, count3[:, :, T - 1:T].rearrange("p e t -> p (e t)")).then_inc(total_ready, 1)
            dve.wait_ge(before_mm, 1)
            link(dve.tensor_copy(before, REC[:, 0:E]))
            link(dve.tensor_tensor(count3, count3, before.unsqueeze(2).broadcast_to([P, E, T]), ALU.add))
            link(dve.tensor_tensor(count, count, onehot_f, ALU.mult))
            link(dve.tensor_reduce(pos, count3.rearrange("p e t -> p t e"), AX.X, ALU.add))
            link(dve.tensor_single_scalar(keep, pos, float(C), ALU.is_le))
            link(dve.tensor_scalar(slot_f, ef, float(C), float(-1 - NSLOT), ALU.mult, ALU.add))
            link(dve.tensor_tensor(slot_f, slot_f, pos, ALU.add))
            link(dve.tensor_tensor(slot_f, slot_f, keep, ALU.mult))
            dve.tensor_scalar(slot_i[:, :], slot_f, float(NSLOT), None, ALU.add).then_inc(slots_ready, 1)

            dve.wait_ge(c_in, 32)
            for i, (dst, src, v) in enumerate(((vr, R[0], V_BR), (vz, Z[0], V_BZ), (vc, H[0], V_BH))):
                dve.wait_ge(v_mm, i + 1)
                for k in range(K):
                    a = dve.tensor_scalar(dst[:, half(k)], src[:, half(k)], vec[:, v, k:k + 1], None, ALU.add)
                a.then_inc(v_ready, 1)
            link(dve.tensor_scalar(leak[:, :], vec[:, V_AL, :], -1.0, 1.0, ALU.mult, ALU.add))
            dve.tensor_copy(leak_t[:, :].rearrange("p (k b) -> p k b", k=K),
                            leak[:, :].unsqueeze(2).broadcast_to([P, K, B])).then_inc(v_ready, 1)
            dve.tensor_copy(b2_t[:, :].rearrange("p (k b) -> p k b", k=K),
                            vec[:, V_B2, :].unsqueeze(2).broadcast_to([P, K, B])).then_inc(v_ready, 1)
            dve.wait_ge(v_ready, 5)

            def add_cond(t, proj, dst, v, ready):
                dve.wait_ge(proj, t + 1)
                dve.tensor_tensor(dst[:, 0:W], dst[:, 0:W], v[:, :], ALU.add).then_inc(ready, 1)

            def mix(t, u, first=False):
                dve.wait_ge(dx_ready, t + 1)
                if not first:
                    dve.wait_ge(tr_mm, t)
                    dve.wait_ge(rec_mm, t)
                for dst, v, ready in ((xr, V_MR, xr_ready), (xk, V_MK, xk_ready)):
                    for k in range(K):
                        a = dve.scalar_tensor_tensor(dst[:, half(k)], dx[:, u, half(k)], vec[:, v, k:k + 1],
                                                     xs[:, at(t + 1, k)], ALU.mult, ALU.add)
                    a.then_inc(ready, 1)

            def step(t, u, first=False, last=False):
                hp, hn = h[:, u, :], h[:, 1 - u, :]
                dve.wait_ge(r_sig, t + 1)
                dve.tensor_tensor(rh[:, :], rg[:, :], hp, ALU.mult).then_inc(rh_ready, 1)
                dve.wait_ge(z_sig, t + 1)
                dve.scalar_tensor_tensor(wh[:, :], zg[:, :], 1.0, hp, ALU.subtract, ALU.mult).then_inc(wh_ready, 1)
                if not last:
                    add_cond(t + 1, r_proj, R[1 - u], vr, rv_ready)
                dve.wait_ge(c_tanh, t + 1)
                dve.tensor_tensor(ph[:, :], zg[:, :], hh[:, :], ALU.mult).then_inc(ph_ready, 1)
                dve.wait_ge(wh_ready, t + 1)
                dve.wait_ge(ph_ready, t + 1)
                if not first:
                    dve.wait_ge(x1_ready, t)
                dve.tensor_tensor(hn, ph[:, :], wh[:, :], ALU.subtract).then_inc(h_ready, 1)
                if not last:
                    add_cond(t + 1, z_proj, Z[1 - u], vz, zv_ready)
                    add_cond(t + 1, c_proj, H[1 - u], vc, cv_ready)
                mix(t, u, first=first)

            add_cond(0, r_proj, R[0], vr, rv_ready)
            add_cond(0, z_proj, Z[0], vz, zv_ready)
            add_cond(0, c_proj, H[0], vc, cv_ready)
            dve.wait_ge(h_ready, 1)
            step(0, 0, first=True)
            step(1, 1)
            with dve.Fori(1, T // 2 - 1) as n:
                step(2 * n, 0)
                step(2 * n + 1, 1)
            step(T - 2, 0)
            step(T - 1, 1, last=True)

            TT = bank[0:2]

            def copy_in(e, first=False):
                for k in range(K):
                    dve.wait_ge(einT_mm, e * K + k + 1)
                    if k == 0 and not first:
                        dve.wait_ge(h_mm, e * FT)
                    dve.tensor_copy(einT[:, k, :], TT[k][:, :]).then_inc(einT_ready, 1)

            def square(e, first=False):
                for f in range(FT):
                    dve.wait_ge(rel_ready, e * FT + f + 1)
                    if f == 0 and not first:
                        dve.wait_ge(o_mm, e * ST)
                    dve.tensor_tensor(hid[:, f, :], hrel[:, f % 2, :], hrel[:, f % 2, :], ALU.mult).then_inc(hid_ready, 1)

            copy_in(0, first=True)
            square(0, first=True)
            copy_in(1)
            with dve.Fori(1, E - 1) as e:
                square(e)
                copy_in(e + 1)
            square(E - 1)

            G, Y = bank[0:2], bank[6:8]
            dve.wait_ge(o_mm, E * ST)
            dve.tensor_copy(h2[:, 0, :], xs[:, 0:W]).then_inc(h2_ready, 1)
            dve.tensor_copy(h3[:, 0, :], xs[:, 0:W]).then_inc(h3_ready, 1)

            def gate_y(t, u):
                dve.wait_ge(yT_mm, t + 1)
                dve.tensor_tensor(rr[:, at(t)], Y[u][:, 0:W], rr[:, at(t)], ALU.mult).then_inc(ry_ready, 1)

            def bias2(t, u):
                dve.wait_ge(g_proj, t + 1)
                dve.tensor_tensor(G[u][:, 0:W], G[u][:, 0:W], b2_t[:, :], ALU.add).then_inc(gb_ready, 1)

            def cstep(t, u, n_left=None):
                if n_left is None or n_left > 1:
                    bias2(t + 1, 1 - u)
                dve.wait_ge(g_sig, t + 1)
                dve.wait_ge(x2_ready, t + 1)
                dve.tensor_tensor(gz[:, :], g2[:, :], xs[:, at(t + 1)], ALU.mult).then_inc(gz_ready, 1)
                dve.wait_ge(gz_ready, t + 1)
                dve.wait_ge(hl_ready, t + 1)
                dve.tensor_tensor(pre[:, :], gz[:, :], hl[:, :], ALU.add).then_inc(pre_ready, 1)
                if n_left is None or n_left > 3:
                    gate_y(t + 3, 1 - u)
                dve.wait_ge(h2_ready, t + 2)
                dve.tensor_tensor(xs[:, at(t + 1)], xs[:, at(t + 1)], h2[:, 1 - u, :], ALU.add).then_inc(x3_ready, 1)

            gate_y(0, 0)
            gate_y(1, 1)
            gate_y(2, 0)
            bias2(0, 0)
            with dve.Fori(0, T // 2 - 2) as n:
                cstep(2 * n, 0)
                cstep(2 * n + 1, 1)
            for t in range(T - 4, T):
                cstep(t, t % 2, n_left=T - t)

        @block.gpsimd
        def _(pool):
            def own_wait():
                pool.wait_ge(zeros_set, 1)

            pool.wait_ge(zeros_set, 1)
            with pool.Fori(0, N_ZFILL) as i:
                pool.dma_start(rows[bass.ds(i * ZROWS, ZROWS), :].rearrange("(p s) d -> p s d", p=P),
                               zeros[:, :].unsqueeze(1).broadcast_to([P, ZROWS // P, D])).then_inc(zfill, 16)
            pool.dma_start(yrows[NSLOT:NSLOT + 1, :], zeros[0:1, :]).then_inc(zfill, 16)

            pool.memset(lower, 1.0).then_inc(const_step, 1)
            pool.memset(ident[:, :], 0.0).then_inc(const_step, 1)
            pool.memset(carry, 1.0).then_inc(const_step, 1)
            pool.iota(eidx, [[1, E], [0, T]], base=0, channel_multiplier=0,
                      allow_small_or_imprecise_dtypes=True).then_inc(consts, 1)
            pool.wait_ge(const_step, 3)
            pool.affine_select(carry.rearrange("p (e t) -> p e t", t=T), carry.rearrange("p (e t) -> p e t", t=T),
                               pattern=[[0, E], [1, T]], compare_op=ALU.is_gt, fill=0.0,
                               base=0, channel_multiplier=0).then_inc(consts, 1)
            pool.affine_select(lower, lower, pattern=[[1, P]], compare_op=ALU.is_gt, fill=0.0,
                               base=0, channel_multiplier=-1).then_inc(consts, 1)
            pool.affine_select(ident[:, :], ident[:, :], pattern=[[-1, P]], compare_op=ALU.not_equal, fill=1.0,
                               base=0, channel_multiplier=1).then_inc(consts, 1)
            pool.wait_ge(slots_ready, 1)
            pool.wait_ge(zfill, 16 * (N_ZFILL + 1))

            last_slot, zero_row = pool.to_reg(NSLOT - 1), pool.to_reg(NSLOT)

            def scatter(t, u, n, first=False):
                if not first:
                    pool.wait_ge(scat[u], n * 16)
                pool.tensor_copy(idx[:, u:u + 1], slot_i[:, bass.ds(t, 1)]).then_inc(idx_ready, 1)
                own_wait()
                pool.wait_ge(idx_ready, t + 1)
                pool.wait_ge(row_ready, t + 1)
                pool.indirect_dma_start(rows, bass.IndirectOffsetOnAxis(idx[:, u:u + 1], axis=0), row[:, u, :], None,
                                        bounds_check=last_slot, oob_is_err=False).then_inc(scat[u], 16)

            def step(t, u, first=False):
                own_wait()
                pool.wait_ge(h_ready, t + 2)
                pool.tensor_tensor(xs[:, at(t + 1)], xs[:, at(t + 1)], h[:, 1 - u, :], ALU.add).then_inc(x1_ready, 1)
                own_wait()
                pool.wait_ge(x1_ready, t + 1)
                if not first:
                    pool.wait_ge(xk_ready, t - 1)
                pool.tensor_tensor(dx[:, u, :], xs[:, at(t)], xs[:, at(t + 1)], ALU.subtract).then_inc(dx_ready, 1)

            step(0, 0, first=True)
            step(1, 1, first=True)
            scatter(0, 0, 0, first=True)
            step(2, 0)
            scatter(1, 1, 0, first=True)
            step(3, 1)
            scatter(2, 0, 1)
            with pool.Fori(2, T // 2) as n:
                step(2 * n, 0)
                scatter(2 * n - 1, 1, n - 1)
                step(2 * n + 1, 1)
                scatter(2 * n, 0, n)
            scatter(T - 1, 1, T // 2 - 1)

            pool.wait_ge(y_out[0], 16 * (E // 2))
            pool.wait_ge(y_out[1], 16 * (E // 2))
            pool.wait_ge(scat[1], 16 * (T // 2))
            pool.wait_ge(scat[0], 16 * (T // 2))

            def gather(t, u, n, first=False):
                if not first:
                    pool.wait_ge(gath[u], n * 16)
                    pool.wait_ge(yT_mm, t - 1)
                pool.tensor_copy(idx[:, u:u + 1], slot_i[:, bass.ds(t, 1)]).then_inc(idy_ready, 1)
                pool.wait_ge(idy_ready, t + 1)
                pool.sem_inc(pool_paced, 1)
                pool.indirect_dma_start(row[:, u, :], None, yrows, bass.IndirectOffsetOnAxis(idx[:, u:u + 1], axis=0),
                                        bounds_check=zero_row, oob_is_err=False).then_inc(gath[u], 16)

            def add_y(t):
                own_wait()
                pool.wait_ge(ry_ready, t + 1)
                pool.tensor_tensor(xs[:, at(t + 1)], xs[:, at(t + 1)], rr[:, at(t)], ALU.add).then_inc(x2_ready, 1)

            def decay(t, u):
                pool.wait_ge(h2_ready, t + 1)
                pool.tensor_tensor(hl[:, :], h2[:, u, :], leak_t[:, :], ALU.mult).then_inc(hl_ready, 1)

            def add_h3(t, u):
                own_wait()
                pool.wait_ge(h3_ready, t + 2)
                pool.tensor_tensor(xs[:, at(t + 1)], xs[:, at(t + 1)], h3[:, 1 - u, :], ALU.add).then_inc(out_ready, 1)

            def cstep(t, u, n, first=False, n_left=None):
                decay(t, u)
                if not first:
                    add_h3(t - 2, u)
                if n_left is None or n_left > 3:
                    add_y(t + 3)
                if n_left is None or n_left > 5:
                    gather(t + 5, 1 - u, n)

            for t in range(2):
                gather(t, t, 0, first=True)
            for t in range(2, 5):
                gather(t, t % 2, t // 2)
            for t in range(3):
                add_y(t)
            cstep(0, 0, 2, first=True)
            cstep(1, 1, 3, first=True)
            with pool.Fori(1, T // 2 - 3) as n:
                cstep(2 * n, 0, n + 2)
                cstep(2 * n + 1, 1, n + 3)
            for t in range(T - 6, T):
                cstep(t, t % 2, (t + 5) // 2, n_left=T - t)
            for t in range(T - 2, T):
                add_h3(t, t % 2)


def _halves(a):
    return a.reshape(K, P, -1).transpose(1, 0, 2)


def kernel(x, cond_1024, itok_BxS_2_50255, L0_cond_W_z, L0_cond_U_z, L0_cond_C_z, L0_cond_b_z, L0_cond_W_r,
           L0_cond_U_r, L0_cond_C_r, L0_cond_b_r, L0_cond_W, L0_cond_U, L0_cond_C, L0_cond_b,
           L1_cond_time_maa_k, L1_cond_time_maa_r, L1_cond_w_recept, L1_cond_w_key, L1_cond_w_value,
           L2_cond_W, L2_cond_b, L2_cond_alpha, L3_cond_Wx, L3_cond_Wh, L3_cond_b):
    import concourse.bacc as bacc
    from concourse.bass_utils import run_bass_kernel_spmd

    a = np.asarray
    l2 = a(L2_cond_W).T
    mats = [L0_cond_W_z, L0_cond_W_r, L0_cond_W, L0_cond_U_z, L0_cond_U_r, L0_cond_U, L0_cond_C_z, L0_cond_C_r,
            L0_cond_C, a(L1_cond_w_recept).T, l2[:D], l2[D:], L3_cond_Wx, L3_cond_Wh]
    vecs = [L0_cond_b_z, L0_cond_b_r, L0_cond_b, L1_cond_time_maa_k, L1_cond_time_maa_r, L2_cond_b, L2_cond_alpha,
            L3_cond_b]
    laid = {
        "x": a(x).reshape(B, T, K, P).transpose(3, 1, 2, 0).reshape(P, T * W),
        "cond": a(cond_1024).reshape(B, K, P).transpose(2, 1, 0).reshape(P, W),
        "ids": a(itok_BxS_2_50255),
        "mats": np.stack([_halves(a(m)) for m in mats], 1),
        "vecs": np.stack([a(v).reshape(K, P).T for v in vecs], 1),
        "w_key": a(L1_cond_w_key).reshape(E, K, P, F).transpose(2, 0, 1, 3).reshape(P, E * K * F),
        "w_value": a(L1_cond_w_value).reshape(E, FT, P, D).transpose(2, 0, 1, 3).reshape(P, E * FT * D),
    }
    laid = {n: np.ascontiguousarray(v) for n, v in laid.items()}

    nc = bacc.Bacc("TRN2", target_bir_lowering=False, num_devices=1)
    args = [nc.dram_tensor(n, v.shape, mybir.dt.from_np(v.dtype), kind="ExternalInput").ap() for n, v in laid.items()]
    out = nc.dram_tensor("out", (P, T * W), F32, kind="ExternalOutput").ap()
    rows = nc.dram_tensor("rows", (NSLOT, D), F32, kind="Internal").ap()
    yrows = nc.dram_tensor("yrows", (NSLOT + 1, D), F32, kind="Internal").ap()
    build(nc, *args, out, rows, yrows)
    r = run_bass_kernel_spmd(nc, [laid], core_ids=[0])
    got = r.results[0]["out"]
    return got.reshape(P, T, K, B).transpose(3, 1, 2, 0).reshape(B, T, D)
```

```python
import numpy as np
from contextlib import ExitStack

import concourse.bass as bass
import concourse.mybir as mybir

F32 = mybir.dt.float32
F32R = mybir.dt.float32r
I32 = mybir.dt.int32
ALU = mybir.AluOpType
ACT = mybir.ActivationFunctionType
AX = mybir.AxisListType

P = 128
B, T, D = 128, 64, 256
K = D // P
W = K * B
NP = T // 2
E, F = 16, 512
C = B * T // E
FT = F // P
ST = C // P
NSLOT = E * C
HASH = 5099 % E
NVEC = 8
V_BZ, V_BR, V_BH, V_MK, V_MR, V_B2, V_AL, V_B3 = range(NVEC)
C_R, C_Z, C_H = range(3)
U_R, U_Z, U_H, L2_H, L3_H = range(5)
S_R, S_Z, S_H, S_REC, S_L2, S_L3 = range(6)
HI, LO = 0, 1
AHEAD = 4
EARLY = 2


def wait_past(eng, sem, count):
    if not isinstance(count, int) or count > 0:
        eng.wait_ge(sem, count)


def exists(m, end=NP, start=0):
    return not isinstance(m, int) or start <= m < end


def build(nc, x, cond, ids, cmats, mats, smats, vecs, w_key, w_value, out, rows, yrows):
    with ExitStack() as ctx:
        scope = [ctx]

        def sb(name, shape, dt=F32):
            return scope[0].enter_context(nc.sbuf_tensor(name, shape, dt))

        def sem(name):
            return ctx.enter_context(nc.semaphore(name))

        bank = [ctx.enter_context(nc.psum_tensor(f"bank{i}", [P, 512], F32)) for i in range(8)]

        def pair_of(bk):
            return bk[:, :].rearrange("p (o s b) -> p o s b", o=K, s=2)

        xs = sb("xs", [P, (T + 1) * W])
        wm = sb("wm", [P, 5, K, D])
        wr = sb("wr", [P, 6, 2, K, D], F32R)
        vec = sb("vec", [P, NVEC, K])
        leak = sb("leak", [P, K])
        leak_t = sb("leak_t", [P, W])
        ident = sb("ident", [P, P])
        slot_i = sb("slot_i", [P, T], I32)
        idx = sb("idx", [P, 4], I32)
        wkv = sb("wkv", [P, 2, 2, K * F])

        ein = sb("ein", [P, 2, ST, D])
        rr = sb("rr", [P, 2, 2 * W])
        dx2 = sb("dx2", [P, 2 * W])
        xr = sb("xr", [P, 2 * W])
        xrs = sb("xrs", [P, 2, 2, K, B], F32R)

        with ExitStack() as phase:
            scope[0] = phase
            wc = sb("wc", [P, 3, K, D])
            zeros = sb("zeros", [P, D])
            onehot = sb("onehot", [P, E, T])
            eidx = sb("eidx", [P, E, T])
            carry = sb("carry", [P, E * T])
            count = sb("count", [P, E * T])
            total, before = sb("total", [P, E]), sb("before", [P, E])
            lower = sb("lower", [P, P])
            id_i = sb("id_i", [P, T], I32)
            ef, pos, keep, slot_f = (sb(n, [P, T]) for n in ("ef", "pos", "keep", "slot_f"))
        scope[0] = ctx
        wkr = sb("wkr", [P, 2, 2, K, F], F32R)
        wvr = sb("wvr", [P, 2, 2, FT, D], F32R)

        with ExitStack() as phase:
            scope[0] = phase
            wsrc = sb("wsrc", [P, 6, K, D])
            v2 = sb("v2", [P, 3, K, 2, B])
            xsp = sb("xsp", [P, 2, 2, 2, K, B], F32R)
            h = sb("h", [P, 2, W])
            rg = sb("rg", [P, K, B])
            zg = sb("zg", [P, K, B])
            hh = sb("hh", [P, K, B])
            wh = sb("wh", [P, W])
            dx = sb("dx", [P, 2, W])
            xk = sb("xk", [P, W])
            row = sb("row", [P, 2, D])
            warm = sb("warm", [P, 1])
        with ExitStack() as phase:
            scope[0] = phase
            einr = sb("einr", [P, 2, K, C], F32R)
            hrel = sb("hrel", [P, 2, C])
            hsq = sb("hsq", [P, C])
            hidr = sb("hidr", [P, 2, FT, C], F32R)
            yo = sb("yo", [P, 2, ST, D])
        with ExitStack() as phase:
            scope[0] = phase
            yrow = sb("yrow", [P, 4, D])
            x2s = sb("x2s", [P, 2, 2, K, B], F32R)
            x3s = sb("x3s", [P, 2, 2, K, B], F32R)
            h2 = sb("h2", [P, 2, W])
            h3 = sb("h3", [P, 4, W])
            g2 = sb("g2", [P, W])
            gz, pre, hl = sb("gz", [P, W]), sb("pre", [P, W]), sb("hl", [P, W])

        x_in, c_in, id_in = sem("x_in"), sem("c_in"), sem("id_in")
        cm_in, um_in, ws_in, wrest_in = sem("cm_in"), sem("um_in"), sem("ws_in"), sem("wrest_in")
        zfill, zeros_set = sem("zfill"), sem("zeros_set")
        consts, const_step, warmed = sem("consts"), sem("const_step"), sem("warmed")
        route_step = sem("route_step")
        total_ready, before_mm, slots_ready = sem("total_ready"), sem("before_mm"), sem("slots_ready")
        v_mm, v_ready = sem("v_mm"), sem("v_ready")
        ws_hi, ws_lo = sem("ws_hi"), sem("ws_lo")
        x_hi, x_lo = sem("x_hi"), sem("x_lo")
        h_ready = sem("h_ready")
        proj_mm = [sem(f"proj_mm_{g}") for g in "rzh"]
        cond_in = [sem(f"cond_in_{g}") for g in "rzh"]
        r_mm, z_mm, c_mm = sem("r_mm"), sem("z_mm"), sem("c_mm")
        r_sig, z_sig, c_tanh = sem("r_sig"), sem("z_sig"), sem("c_tanh")
        rh_ready, wh_ready, ph_ready = sem("rh_ready"), sem("wh_ready"), sem("ph_ready")
        x1_ready, dx_ready, xk_ready = sem("x1_ready"), sem("dx_ready"), sem("xk_ready")
        tr_mm, row_ready, idx_ready = sem("tr_mm"), sem("row_ready"), sem("idx_ready")
        scat = [sem("scat0"), sem("scat1")]
        kv_in = [sem("kv_in0"), sem("kv_in1")]
        ein_in = [sem("ein_in0"), sem("ein_in1")]
        w_hi, w_lo = sem("w_hi"), sem("w_lo")
        einT_mm, ein_hi, ein_lo = sem("einT_mm"), sem("ein_hi"), sem("ein_lo")
        h_mm, rel_ready, sq_ready = sem("h_mm"), sem("rel_ready"), sem("sq_ready")
        hid_hi, hid_lo = sem("hid_hi"), sem("hid_lo")
        o_mm, o_ready = sem("o_mm"), sem("o_ready")
        y_out = [sem("y_out0"), sem("y_out1")]
        idy_ready = sem("idy_ready")
        gath = [sem(f"gath{i}") for i in range(4)]
        dx2_ready, xr_ready, xr_hi, xr_lo = sem("dx2_ready"), sem("xr_ready"), sem("xr_hi"), sem("xr_lo")
        rec_mm, rec_sig, yT_mm, ry_ready = sem("rec_mm"), sem("rec_sig"), sem("yT_mm"), sem("ry_ready")
        x2_ready, x2_hi, x2_lo = sem("x2_ready"), sem("x2_hi"), sem("x2_lo")
        x3_ready, x3_hi, x3_lo = sem("x3_ready"), sem("x3_hi"), sem("x3_lo")
        x2_used, x3_used = sem("x2_used"), sem("x3_used")
        h2_ready, h3_ready, hl_ready = sem("h2_ready"), sem("h3_ready"), sem("hl_ready")
        g_mm, g_sig, gz_ready, pre_ready = sem("g_mm"), sem("g_sig"), sem("gz_ready"), sem("pre_ready")
        p3_mm, out_ready, stored = sem("p3_mm"), sem("out_ready"), sem("stored")
        pool_paced = sem("pool_paced")

        FIRST = 4
        ZPARTS = 4
        ZR = NSLOT // ZPARTS

        def at(t):
            return bass.ds(t * W + W, W)

        def pair(n, before=0):
            return bass.ds(n * 2 * W + (1 - before) * W, 2 * W)

        def half(k):
            return slice(k * B, (k + 1) * B)

        def split_of(tile):
            return lambda c, k: tile[:, c, :, k, :]

        block = ctx.enter_context(nc.Block())

        @block.sync
        def _(sp):
            sp.dma_start(xs[:, 0:W], cond).then_inc(c_in, 16)
            sp.dma_start(vec[:, :, :], vecs).then_inc(c_in, 16)
            sp.dma_start(xs[:, pair(0)], x[:, 0:2 * W]).then_inc(x_in, 16)
            sp.dma_start(wsrc[:, 0:3, :, :], smats[:, 0:3, :, :]).then_inc(ws_in, 16)
            sp.dma_start(wm[:, U_R:U_H + 1, :, :], mats[:, U_R:U_H + 1, :, :]).then_inc(um_in, 16)
            for n in range(1, FIRST):
                sp.wait_ge(x_in, n * 16)
                sp.dma_start(xs[:, pair(n)], x[:, n * 2 * W:(n + 1) * 2 * W]).then_inc(x_in, 16)
            sp.wait_ge(zeros_set, 1)
            for i in range(ZPARTS):
                sp.dma_start(rows[i * ZR:(i + 1) * ZR, :].rearrange("(p s) d -> p s d", p=P),
                             zeros[:, :].unsqueeze(1).broadcast_to([P, ZR // P, D])).then_inc(zfill, 16)
            sp.dma_start(yrows[NSLOT:NSLOT + 1, :], zeros[0:1, :]).then_inc(zfill, 16)
            with sp.Fori(FIRST, NP) as n:
                sp.wait_ge(x_in, n * 16)
                sp.dma_start(xs[:, pair(n)], x[:, bass.ds(n * 2 * W, 2 * W)]).then_inc(x_in, 16)

            sp.dma_start(wsrc[:, 3:6, :, :], smats[:, 3:6, :, :]).then_inc(wrest_in, 16)
            sp.dma_start(wm[:, L2_H:L3_H + 1, :, :], mats[:, L2_H:L3_H + 1, :, :]).then_inc(wrest_in, 16)

            def load_kv(e, u):
                sp.dma_start(wkv[:, u, 0, :], w_key[:, bass.ds(e * K * F, K * F)]).then_inc(kv_in[u], 16)
                sp.dma_start(wkv[:, u, 1, :], w_value[:, bass.ds(e * FT * D, FT * D)]).then_inc(kv_in[u], 16)

            def load_rows(e, u):
                sp.dma_start(ein[:, u, :, :],
                             rows[bass.ds(e * C, C), :].rearrange("(s p) d -> p s d", p=P)).then_inc(ein_in[u], 16)

            def store(e, u):
                sp.wait_ge(o_ready, (e + 1) * 2)
                sp.dma_start(yrows[bass.ds(e * C, C), :].rearrange("(s p) d -> p s d", p=P),
                             yo[:, u, :, :]).then_inc(y_out[u], 16)

            load_kv(0, 0)
            load_kv(1, 1)
            sp.wait_ge(scat[0], 16 * NP)
            sp.wait_ge(scat[1], 16 * NP)
            load_rows(0, 0)
            load_rows(1, 1)
            with sp.Fori(1, E // 2) as n:
                for u in range(2):
                    sp.wait_ge(w_lo, (2 * n + u - 1) * 2)
                    load_kv(2 * n + u, u)
                    sp.wait_ge(einT_mm, (2 * n + u - 1) * K)
                    load_rows(2 * n + u, u)
                    store(2 * n + u - 2, u)
            for e in range(E - 2, E):
                store(e, e % 2)
            with sp.Fori(0, NP) as n:
                sp.wait_ge(out_ready, n + 1)
                sp.dma_start(out[:, bass.ds(n * 2 * W, 2 * W)], xs[:, pair(n)]).then_inc(stored, 16)
            sp.wait_ge(stored, 16 * NP)

        @block.tensor
        def _(pe):
            gates = [bank[0:2], bank[2:4], bank[4:6]]
            MISC, TR = bank[6], bank[7]

            def prod32(dst, w, rhs, start):
                for o in range(K):
                    for k in range(K):
                        mm = pe.matmul(dst(o), w[:, k, o * P:(o + 1) * P], rhs(k),
                                       start=start and o == 0 and k == 0, stop=k == K - 1, skip_group_check=True)
                return mm

            def prod_split(bk, m, rhs, first=0, last=6 * K):
                passes = [(o, k, a, b) for o in range(K) for k in range(K) for a, b in ((HI, HI), (HI, LO), (LO, HI))]
                for o, k, a, b in passes[first:last]:
                    mm = pe.matmul(pair_of(bk)[:, o, :, :], wr[:, m, a, k, o * P:(o + 1) * P], rhs(b, k),
                                   start=(o, k, a, b) == (0, 0, HI, HI), stop=False, skip_group_check=True)
                return mm

            def step_of(bk, s):
                return lambda o: pair_of(bk)[:, o, s, :]

            pe.wait_ge(c_in, 32)
            pe.wait_ge(cm_in, 16)
            for g, m in enumerate((C_R, C_Z, C_H)):
                prod32(lambda o: gates[g][1][:, half(o)], wc[:, m, :, :], lambda k: xs[:, half(k)], True).then_inc(v_mm, 1)
                if g == 0:
                    pe.wait_ge(consts, 4)
                    pe.wait_ge(total_ready, 1)
                    pe.matmul(MISC[:, 0:E], lower[:, :], total[:, :], start=True, stop=True).then_inc(before_mm, 1)

            def turn_rows(t):
                pe.wait_ge(xk_ready, t + 1)
                wait_past(pe, row_ready, t)
                for k in range(K):
                    mm = pe.transpose(TR[:, k * P:(k + 1) * P], xk[:, half(k)], ident[:, :])
                mm.then_inc(tr_mm, 1)

            def pair_a(n, q):
                xn = split_of(xsp[:, 1 - q, :, :, :, :])
                for s in range(2):
                    t = 2 * n + s
                    pe.wait_ge(h_ready, t + 1)
                    more = exists(n + 1)
                    for g, (m, done) in enumerate(((U_R, r_mm), (U_Z, z_mm), (U_H, c_mm))):
                        if s == 0:
                            pe.wait_ge(cond_in[g], n + 1)
                        if g == 2:
                            if more and s == 0:
                                pe.wait_ge(x_lo, n + 2)
                                prod_split(gates[0][1 - q], S_R, xn, 0, 4)
                            if more and s == 1:
                                prod_split(gates[1][1 - q], S_Z, xn, 6, 10)
                            pe.wait_ge(rh_ready, t + 1)
                        rhs = (lambda k: rg[:, k, :]) if g == 2 else (lambda k: h[:, s, half(k)])
                        prod32(step_of(gates[g][q], s), wm[:, m, :, :], rhs, False).then_inc(done, 1)
                    if more and s == 0:
                        prod_split(gates[0][1 - q], S_R, xn, 4).then_inc(proj_mm[0], 1)
                        prod_split(gates[1][1 - q], S_Z, xn, 0, 6)
                    if more and s == 1:
                        prod_split(gates[1][1 - q], S_Z, xn, 10).then_inc(proj_mm[1], 1)
                        prod_split(gates[2][1 - q], S_H, xn).then_inc(proj_mm[2], 1)
                    if exists(t - 1, end=T):
                        turn_rows(t - 1)

            pe.wait_ge(x_lo, 1)
            for g, m in enumerate((S_R, S_Z, S_H)):
                pe.wait_ge(ws_lo, g + 1)
                prod_split(gates[g][0], m, split_of(xsp[:, 0, :, :, :, :])).then_inc(proj_mm[g], 1)
            pe.wait_ge(um_in, 16)
            pe.wait_ge(v_ready, 3)
            pair_a(0, 0)
            pair_a(1, 1)
            with pe.Fori(1, NP // 2 - 1) as i:
                pair_a(2 * i, 0)
                pair_a(2 * i + 1, 1)
            pair_a(NP - 2, 0)
            pair_a(NP - 1, 1)
            turn_rows(T - 1)

            REC = bank[4]

            def receptance(n):
                pe.wait_ge(xr_lo, n + 1)
                wait_past(pe, rec_sig, n)
                prod_split(REC, S_REC, split_of(xrs)).then_inc(rec_mm, 1)

            TT, HB, OB = bank[0:2], bank[2:4], bank[4:8]

            def turn_in(e, u, n):
                pe.wait_ge(ein_in[u], (n + 1) * 16)
                wait_past(pe, ein_lo, e * K)
                for k in range(K):
                    for s in range(ST):
                        mm = pe.transpose(TT[k][:, s * P:(s + 1) * P], ein[:, u, s, k * P:(k + 1) * P], ident[:, :])
                    mm.then_inc(einT_mm, 1)

            def hidden(e, u):
                pe.wait_ge(ein_lo, (e + 1) * K)
                pe.wait_ge(w_lo, e * 2 + 1)
                for f in range(FT):
                    wait_past(pe, rel_ready, e * FT + f - 1)
                    for k in range(K):
                        for a, b in ((HI, HI), (HI, LO), (LO, HI)):
                            mm = pe.matmul(HB[f % 2][:, :], wkr[:, u, a, k, f * P:(f + 1) * P], einr[:, b, k, :],
                                           start=k == 0 and (a, b) == (HI, HI), stop=k == K - 1 and a == LO)
                    mm.then_inc(h_mm, 1)

            def project(e, u):
                pe.wait_ge(w_lo, (e + 1) * 2)
                wait_past(pe, o_ready, (e - 1) * 2)
                for f in range(FT):
                    pe.wait_ge(hid_lo, e * FT + f + 1)
                    for s in range(ST):
                        for a, b in ((HI, HI), (HI, LO), (LO, HI)):
                            mm = pe.matmul(OB[2 * u + s // 2][:, (s % 2) * D:(s % 2 + 1) * D],
                                           hidr[:, a, f, s * P:(s + 1) * P], wvr[:, u, b, f, :],
                                           start=f == 0 and s % 2 == 0 and (a, b) == (HI, HI),
                                           stop=f == FT - 1 and a == LO, skip_group_check=True)
                mm.then_inc(o_mm, 1)

            def experts(i, last=False):
                for u in range(2):
                    hidden(2 * i + u, u)
                    if not (last and u):
                        turn_in(2 * i + u + 1, 1 - u, i + u)
                    project(2 * i + u, u)

            for n in range(EARLY):
                receptance(n)
            turn_in(0, 0, 0)
            pe.wait_ge(rec_sig, EARLY)
            experts(0)
            with pe.Fori(1, E // 2 - 1) as i:
                experts(i)
            experts(E // 2 - 1, last=True)

            G, Q, Y = bank[0:2], bank[2:4], bank[6:8]

            def turn_y(n, q, count):
                wait_past(pe, ry_ready, n - 1)
                for s in range(2):
                    pe.wait_ge(gath[2 * q + s], count * 16)
                    for k in range(K):
                        mm = pe.transpose(Y[q][:, s * W + k * B:s * W + (k + 1) * B],
                                          yrow[:, 2 * q + s, k * P:(k + 1) * P], ident[:, :])
                mm.then_inc(yT_mm, 1)

            def proj2(n, q):
                pe.wait_ge(x2_lo, n + 1)
                prod_split(G[q], S_L2, split_of(x2s)).then_inc(x2_used, 1)

            def proj3(n, q):
                pe.wait_ge(x3_lo, n + 1)
                prod_split(Q[q], S_L3, split_of(x3s)).then_inc(x3_used, 1)

            def step3(t, q, s):
                pe.wait_ge(h3_ready, t + 1)
                prod32(step_of(Q[q], s), wm[:, L3_H, :, :], lambda k: h3[:, (2 * q + s - 1) % 4, half(k)], False).then_inc(p3_mm, 1)

            def step2(t, q, s):
                pe.wait_ge(h2_ready, t + 1)
                prod32(step_of(G[q], s), wm[:, L2_H, :, :], lambda k: h2[:, 1 - s, half(k)], False).then_inc(g_mm, 1)

            def pair_c(n, q, i):
                if exists(n):
                    step2(2 * n, q, 0)
                if exists(n + 1):
                    proj2(n + 1, 1 - q)
                if exists(n + 3):
                    turn_y(n + 3, 1 - q, i + 2 + q)
                if exists(n - 2):
                    step3(2 * n - 3, q, 1)
                if exists(n):
                    step2(2 * n + 1, q, 1)
                if exists(n - 1):
                    proj3(n - 1, 1 - q)
                if exists(n + 3, start=EARLY):
                    receptance(n + 3)
                if exists(n - 1):
                    step3(2 * n - 2, 1 - q, 0)

            pe.wait_ge(o_ready, E * 2)
            for n in range(-AHEAD, 4):
                pair_c(n, n % 2, n // 2)
            with pe.Fori(2, NP // 2 - 2) as i:
                pair_c(2 * i, 0, i)
                pair_c(2 * i + 1, 1, i)
            for n in range(NP - AHEAD, NP + 2):
                pair_c(n, n % 2, n // 2)

        @block.scalar
        def _(act):
            def own_wait():
                act.wait_ge(zeros_set, 1)

            act.dma_start(id_i[:, :], ids).then_inc(id_in, 16)
            act.dma_start(wc[:, :, :, :], cmats).then_inc(cm_in, 16)
            act.wait_ge(zeros_set, 1)
            act.activation(warm[:, :], zeros[:, 0:1], ACT.Sigmoid).then_inc(warmed, 1)

            gates = [bank[0:2], bank[2:4], bank[4:6]]
            TR = bank[7]

            def split_matrix(m):
                act.activation(wr[:, m, HI, :, :], wsrc[:, m, :, :], ACT.Copy).then_inc(ws_hi, 1)

            def split_x(n, q):
                own_wait()
                act.wait_ge(x_in, (n + 1) * 16)
                wait_past(act, proj_mm[2], n - 1)
                act.activation(xsp[:, q, HI, :, :, :].rearrange("p s k b -> p (s k b)"),
                               xs[:, pair(n)], ACT.Copy).then_inc(x_hi, 1)

            def row_out(t, u, sent):
                act.wait_ge(tr_mm, t + 1)
                wait_past(act, scat[u], sent * 16)
                act.activation(row[:, u, :], TR[:, 0:D], ACT.Copy).then_inc(row_ready, 1)

            def pair_a(n, q):
                for s in range(2):
                    t = 2 * n + s
                    for g, (dst, f, mm, done) in enumerate(((rg, ACT.Sigmoid, r_mm, r_sig),
                                                            (zg, ACT.Sigmoid, z_mm, z_sig),
                                                            (hh, ACT.Tanh, c_mm, c_tanh))):
                        act.wait_ge(mm, t + 1)
                        act.activation(dst[:, :, :], pair_of(gates[g][q])[:, :, s, :], f).then_inc(done, 1)
                        if g == 1 and s == 0 and exists(n + 2):
                            split_x(n + 2, q)
                    if exists(t - 1, end=T):
                        row_out(t - 1, 1 - s, n - 1 + s)

            split_x(0, 0)
            act.wait_ge(ws_in, 16)
            for m in range(3):
                split_matrix(m)
            split_x(1, 1)
            pair_a(0, 0)
            pair_a(1, 1)
            with act.Fori(1, NP // 2 - 1) as i:
                pair_a(2 * i, 0)
                pair_a(2 * i + 1, 1)
            act.wait_ge(wrest_in, 32)
            split_matrix(3)
            pair_a(NP - 2, 0)
            split_matrix(4)
            split_matrix(5)
            pair_a(NP - 1, 1)
            row_out(T - 1, 1, NP - 1)

            REC = bank[4]
            act.wait_ge(slots_ready, 1)
            act.wait_ge(v_ready, 3)
            act.wait_ge(zfill, 16 * (ZPARTS + 1))
            act.wait_ge(kv_in[0], 32)
            for j, wide in enumerate((wkr, wvr)):
                act.activation(wide[:, 0, HI, :, :].rearrange("p a b -> p (a b)"), wkv[:, 0, j, :], ACT.Copy)\
                   .then_inc(w_hi, 1)

            def flat(t, c):
                return t[:, c, :, :, :].rearrange("p s k b -> p (s k b)")

            def high_xr(n):
                act.wait_ge(xr_ready, n + 1)
                act.activation(flat(xrs, HI), xr[:, :], ACT.Copy).then_inc(xr_hi, 1)

            def receptance(n, q):
                act.wait_ge(rec_mm, n + 1)
                act.activation(rr[:, q, :].rearrange("p (s k b) -> p k s b", s=2, k=K), pair_of(REC), ACT.Sigmoid)\
                   .then_inc(rec_sig, 1)

            for n in range(EARLY):
                high_xr(n)
                receptance(n, n % 2)

            TT, HB, OB = bank[0:2], bank[2:4], bank[4:8]

            def split_in(e):
                for k in range(K):
                    act.wait_ge(einT_mm, e * K + k + 1)
                    if k == 0:
                        wait_past(act, h_mm, e * FT)
                    act.activation(einr[:, HI, k, :], TT[k][:, :], ACT.Copy).then_inc(ein_hi, 1)

            def expert(e, u, sent, last=False):
                for f in range(FT):
                    act.wait_ge(h_mm, e * FT + f + 1)
                    wait_past(act, sq_ready, e * FT + f - 1)
                    act.activation(hrel[:, f % 2, :], HB[f % 2][:, :], ACT.Relu).then_inc(rel_ready, 1)
                if not last:
                    split_in(e + 1)
                act.wait_ge(o_mm, e + 1)
                wait_past(act, y_out[u], sent * 16)
                for j in range(2):
                    act.activation(yo[:, u, 2 * j:2 * j + 2, :].rearrange("p s d -> p (s d)"),
                                   OB[2 * u + j][:, :], ACT.Copy).then_inc(o_ready, 1)

            split_in(0)
            expert(0, 0, 0)
            expert(1, 1, 0)
            with act.Fori(1, E // 2 - 1) as i:
                expert(2 * i, 0, i)
                expert(2 * i + 1, 1, i)
            expert(E - 2, 0, E // 2 - 1)
            expert(E - 1, 1, E // 2 - 1, last=True)

            G, Q = bank[0:2], bank[2:4]

            def high_x2(n):
                own_wait()
                act.wait_ge(x2_ready, n + 1)
                wait_past(act, x2_used, n)
                act.activation(flat(x2s, HI), xs[:, pair(n)], ACT.Copy).then_inc(x2_hi, 1)

            def high_x3(n):
                own_wait()
                act.wait_ge(x3_ready, 2 * n + 2)
                wait_past(act, x3_used, n)
                act.activation(flat(x3s, HI), xs[:, pair(n)], ACT.Copy).then_inc(x3_hi, 1)

            def gate2(t, q, s):
                act.wait_ge(g_mm, t + 1)
                for k in range(K):
                    a = act.activation(g2[:, half(k)], pair_of(G[q])[:, k, s, :], ACT.Sigmoid,
                                       bias=vec[:, V_B2, k:k + 1])
                a.then_inc(g_sig, 1)

            def state2(t, s):
                act.wait_ge(pre_ready, t + 1)
                act.activation(h2[:, s, :], pre[:, :], ACT.Tanh).then_inc(h2_ready, 1)

            def state3(t, q, s, n):
                act.wait_ge(p3_mm, t + 1)
                wait_past(act, out_ready, n - 1)
                for k in range(K):
                    a = act.activation(h3[:, 2 * q + s, half(k)], pair_of(Q[q])[:, k, s, :], ACT.Tanh,
                                       bias=vec[:, V_B3, k:k + 1])
                a.then_inc(h3_ready, 1)

            def pair_c(n, q):
                if exists(n - 1):
                    high_x3(n - 1)
                if exists(n):
                    gate2(2 * n, q, 0)
                if exists(n - 2):
                    state3(2 * n - 4, q, 0, n - 2)
                if exists(n):
                    state2(2 * n, 0)
                if exists(n + 3, start=EARLY):
                    high_xr(n + 3)
                if exists(n - 2):
                    state3(2 * n - 3, q, 1, n - 2)
                if exists(n):
                    gate2(2 * n + 1, q, 1)
                if exists(n + 2):
                    high_x2(n + 2)
                if exists(n):
                    state2(2 * n + 1, 1)
                if exists(n + 3, start=EARLY):
                    receptance(n + 3, 1 - q)

            for n in range(-AHEAD, 4):
                pair_c(n, n % 2)
            with act.Fori(2, NP // 2 - 2) as i:
                pair_c(2 * i, 0)
                pair_c(2 * i + 1, 1)
            for n in range(NP - AHEAD, NP + 2):
                pair_c(n, n % 2)

        @block.vector
        def _(dve):
            gates = [bank[0:2], bank[2:4], bank[4:6]]
            MISC = bank[6]
            dve.memset(zeros[:, :], 0.0).then_inc(zeros_set, 1)
            dve.memset(h[:, 0, :], 0.0).then_inc(h_ready, 1)

            chain = [0]

            def link(ins):
                chain[0] += 1
                ins.then_inc(route_step, 1)
                dve.wait_ge(route_step, chain[0])

            def route():
                dve.wait_ge(id_in, 16)
                link(dve.tensor_single_scalar(id_i[:, :], id_i[:, :], E - 1, ALU.bitwise_and))
                link(dve.tensor_single_scalar(id_i[:, :], id_i[:, :], float(HASH), ALU.mult))
                link(dve.tensor_single_scalar(id_i[:, :], id_i[:, :], E - 1, ALU.bitwise_and))
                link(dve.tensor_copy(ef[:, :], id_i[:, :]))
                dve.wait_ge(consts, 1)
                link(dve.tensor_tensor(onehot[:, :, :], eidx[:, :, :],
                                       ef[:, :].unsqueeze(1).broadcast_to([P, E, T]), ALU.is_equal))
                dve.wait_ge(consts, 2)
                link(dve.tensor_tensor_scan(count[:, :], carry[:, :], onehot[:, :, :].rearrange("p e t -> p (e t)"),
                                            0.0, ALU.mult, ALU.add))
                count3 = count[:, :].rearrange("p (e t) -> p e t", t=T)
                dve.tensor_copy(total[:, :], count3[:, :, T - 1:T].rearrange("p e t -> p (e t)"))\
                   .then_inc(total_ready, 1)

            def place():
                count3 = count[:, :].rearrange("p (e t) -> p e t", t=T)
                dve.wait_ge(before_mm, 1)
                link(dve.tensor_copy(before[:, :], MISC[:, 0:E]))
                link(dve.tensor_tensor(count3, count3, before[:, :].unsqueeze(2).broadcast_to([P, E, T]), ALU.add))
                link(dve.tensor_tensor(count3, count3, onehot[:, :, :], ALU.mult))
                link(dve.tensor_reduce(pos[:, :], count3.rearrange("p e t -> p t e"), AX.X, ALU.add))
                link(dve.tensor_single_scalar(keep[:, :], pos[:, :], float(C), ALU.is_le))
                link(dve.tensor_scalar(slot_f[:, :], ef[:, :], float(C), float(-1 - NSLOT), ALU.mult, ALU.add))
                link(dve.tensor_tensor(slot_f[:, :], slot_f[:, :], pos[:, :], ALU.add))
                link(dve.tensor_tensor(slot_f[:, :], slot_f[:, :], keep[:, :], ALU.mult))
                dve.tensor_scalar(slot_i[:, :], slot_f[:, :], float(NSLOT), None, ALU.add).then_inc(slots_ready, 1)

            def low(dst, src, high, done):
                dve.tensor_tensor(dst, src, high.bitcast(F32), ALU.subtract).then_inc(done, 1)

            def low_matrix(m):
                dve.wait_ge(ws_hi, m + 1)
                low(wr[:, m, LO, :, :], wsrc[:, m, :, :], wr[:, m, HI, :, :], ws_lo)

            def low_x(n, q):
                dve.wait_ge(x_hi, n + 1)
                f = [xsp[:, q, c, :, :, :].rearrange("p s k b -> p (s k b)") for c in (HI, LO)]
                low(f[LO], xs[:, pair(n)], f[HI], x_lo)

            route()
            place()
            low_x(0, 0)
            for m in range(3):
                low_matrix(m)
            dve.wait_ge(c_in, 32)
            for g, v in enumerate((V_BR, V_BZ, V_BH)):
                dve.wait_ge(v_mm, g + 1)
                for k in range(K):
                    a = dve.tensor_scalar(v2[:, g, k, :, :],
                                          gates[g][1][:, half(k)].unsqueeze(1).broadcast_to([P, 2, B]),
                                          vec[:, v, k:k + 1], None, ALU.add)
                a.then_inc(v_ready, 1)
            dve.wait_ge(v_ready, 3)

            def add_cond(g, n, q):
                dve.wait_ge(proj_mm[g], n + 1)
                bk = gates[g][q]
                dve.tensor_tensor(bk[:, :], bk[:, :], v2[:, g, :, :, :].rearrange("p k s b -> p (k s b)"),
                                  ALU.add).then_inc(cond_in[g], 1)

            for g in range(3):
                add_cond(g, 0, 0)
            low_x(1, 1)

            def mix(t, u):
                dve.wait_ge(dx_ready, t + 1)
                wait_past(dve, tr_mm, t)
                for k in range(K):
                    a = dve.scalar_tensor_tensor(xk[:, half(k)], dx[:, u, half(k)], vec[:, V_MK, k:k + 1],
                                                 xs[:, bass.ds(t * W + W + k * B, B)], ALU.mult, ALU.add)
                a.then_inc(xk_ready, 1)

            def pair_a(n, q):
                for s in range(2):
                    t = 2 * n + s
                    hp, hn = h[:, s, :], h[:, 1 - s, :]
                    dve.wait_ge(h_ready, t + 1)
                    dve.wait_ge(r_sig, t + 1)
                    r = rg[:, :, :].rearrange("p k b -> p (k b)")
                    dve.tensor_tensor(r, r, hp, ALU.mult)\
                       .then_inc(rh_ready, 1)
                    z = zg[:, :, :].rearrange("p k b -> p (k b)")
                    dve.wait_ge(z_sig, t + 1)
                    dve.scalar_tensor_tensor(wh[:, :], z, 1.0, hp, ALU.subtract, ALU.mult).then_inc(wh_ready, 1)
                    if exists(t - 1, end=T):
                        mix(t - 1, 1 - s)
                    dve.wait_ge(c_tanh, t + 1)
                    c = hh[:, :, :].rearrange("p k b -> p (k b)")
                    dve.tensor_tensor(c, z, c, ALU.mult)\
                       .then_inc(ph_ready, 1)
                    dve.wait_ge(wh_ready, t + 1)
                    dve.wait_ge(ph_ready, t + 1)
                    wait_past(dve, x1_ready, t)
                    dve.tensor_tensor(hn, c, wh[:, :], ALU.subtract).then_inc(h_ready, 1)
                    if exists(n + 1):
                        if s == 0:
                            add_cond(0, n + 1, 1 - q)
                        else:
                            add_cond(1, n + 1, 1 - q)
                            add_cond(2, n + 1, 1 - q)
                    if s == 0 and exists(n + 2):
                        low_x(n + 2, q)

            pair_a(0, 0)
            link(dve.tensor_scalar(leak[:, :], vec[:, V_AL, :], -1.0, 1.0, ALU.mult, ALU.add))
            dve.tensor_copy(leak_t[:, :].rearrange("p (k b) -> p k b", k=K),
                            leak[:, :].unsqueeze(2).broadcast_to([P, K, B])).then_inc(v_ready, 1)
            pair_a(1, 1)
            with dve.Fori(1, NP // 2 - 1) as i:
                pair_a(2 * i, 0)
                pair_a(2 * i + 1, 1)
            low_matrix(3)
            pair_a(NP - 2, 0)
            low_matrix(4)
            low_matrix(5)
            pair_a(NP - 1, 1)
            mix(T - 1, 1)

            for j, wide in enumerate((wkr, wvr)):
                part = [wide[:, 0, c, :, :].rearrange("p a b -> p (a b)") for c in (HI, LO)]
                dve.wait_ge(w_hi, j + 1)
                low(part[LO], wkv[:, 0, j, :], part[HI], w_lo)

            def flat(t, c):
                return t[:, c, :, :, :].rearrange("p s k b -> p (s k b)")

            def mix_r(n):
                wait_past(dve, xr_lo, n)
                dve.wait_ge(dx2_ready, n + 1)
                xr3, dx3 = (v[:, :].rearrange("p (s k b) -> p s k b", s=2, k=K) for v in (xr, dx2))
                x3 = xs[:, pair(n)].rearrange("p (s k b) -> p s k b", s=2, k=K)
                for k in range(K):
                    a = dve.scalar_tensor_tensor(xr3[:, :, k, :], dx3[:, :, k, :], vec[:, V_MR, k:k + 1],
                                                 x3[:, :, k, :], ALU.mult, ALU.add)
                a.then_inc(xr_ready, 1)

            def low_xr(n):
                dve.wait_ge(xr_hi, n + 1)
                low(flat(xrs, LO), xr[:, :], flat(xrs, HI), xr_lo)

            mix_r(0)
            for n in range(EARLY):
                low_xr(n)
                mix_r(n + 1)

            TT = bank[0:2]

            def low_in(e):
                for k in range(K):
                    dve.wait_ge(ein_hi, e * K + k + 1)
                    low(einr[:, LO, k, :], TT[k][:, :], einr[:, HI, k, :], ein_lo)

            def expert(e, last=False):
                for f in range(FT):
                    dve.wait_ge(rel_ready, e * FT + f + 1)
                    if f == 0:
                        wait_past(dve, o_mm, e)
                    sq = hsq[:, :]
                    wait_past(dve, hid_lo, e * FT + f)
                    dve.tensor_tensor(sq, hrel[:, f % 2, :], hrel[:, f % 2, :], ALU.mult).then_inc(sq_ready, 1)
                    dve.wait_ge(sq_ready, e * FT + f + 1)
                    dve.tensor_copy(hidr[:, HI, f, :], sq).then_inc(hid_hi, 1)
                    dve.wait_ge(hid_hi, e * FT + f + 1)
                    low(hidr[:, LO, f, :], sq, hidr[:, HI, f, :], hid_lo)
                if not last:
                    low_in(e + 1)

            low_in(0)
            expert(0)
            with dve.Fori(1, E - 1) as e:
                expert(e)
            expert(E - 1, last=True)

            Y = bank[6:8]
            dve.wait_ge(y_out[0], 16 * (E // 2))
            dve.wait_ge(y_out[1], 16 * (E // 2))
            dve.tensor_copy(h2[:, 1, :], xs[:, 0:W]).then_inc(h2_ready, 1)
            dve.tensor_copy(h3[:, 3, :], xs[:, 0:W]).then_inc(h3_ready, 1)

            def gate_y(n, q):
                dve.wait_ge(yT_mm, n + 1)
                dve.wait_ge(rec_sig, n + 1)
                dve.tensor_tensor(rr[:, q, :], Y[q][:, :], rr[:, q, :], ALU.mult).then_inc(ry_ready, 1)

            def low_x2(n):
                dve.wait_ge(x2_hi, n + 1)
                low(flat(x2s, LO), xs[:, pair(n)], flat(x2s, HI), x2_lo)

            def low_x3(n):
                dve.wait_ge(x3_hi, n + 1)
                low(flat(x3s, LO), xs[:, pair(n)], flat(x3s, HI), x3_lo)

            def decay(t, s):
                dve.wait_ge(h2_ready, t + 1)
                dve.tensor_tensor(hl[:, :], h2[:, 1 - s, :], leak_t[:, :], ALU.mult).then_inc(hl_ready, 1)

            def inner(t):
                dve.wait_ge(g_sig, t + 1)
                dve.tensor_tensor(gz[:, :], g2[:, :], xs[:, at(t)], ALU.mult).then_inc(gz_ready, 1)
                dve.wait_ge(gz_ready, t + 1)
                dve.wait_ge(hl_ready, t + 1)
                dve.tensor_tensor(pre[:, :], gz[:, :], hl[:, :], ALU.add).then_inc(pre_ready, 1)

            def add_h2(t, s):
                dve.wait_ge(h2_ready, t + 2)
                dve.tensor_tensor(xs[:, at(t)], xs[:, at(t)], h2[:, s, :], ALU.add).then_inc(x3_ready, 1)

            def pair_c(n, q):
                if exists(n - 1):
                    low_x3(n - 1)
                if exists(n):
                    inner(2 * n)
                if exists(n + 2):
                    gate_y(n + 2, q)
                if exists(n):
                    add_h2(2 * n, 0)
                    decay(2 * n + 1, 1)
                if exists(n + 3, start=EARLY):
                    low_xr(n + 3)
                if exists(n + 4, start=EARLY + 1):
                    mix_r(n + 4)
                if exists(n):
                    inner(2 * n + 1)
                if exists(n + 2):
                    low_x2(n + 2)
                if exists(n):
                    add_h2(2 * n + 1, 1)
                if exists(n + 1):
                    decay(2 * n + 2, 0)

            for n in range(-AHEAD, 4):
                pair_c(n, n % 2)
            with dve.Fori(2, NP // 2 - 2) as i:
                pair_c(2 * i, 0)
                pair_c(2 * i + 1, 1)
            for n in range(NP - AHEAD, NP + 2):
                pair_c(n, n % 2)

        @block.gpsimd
        def _(pool):
            def own_wait():
                pool.wait_ge(zeros_set, 1)

            pool.iota(eidx[:, :, :], [[1, E], [0, T]], base=0, channel_multiplier=0,
                      allow_small_or_imprecise_dtypes=True).then_inc(consts, 1)
            pool.memset(carry[:, :], 1.0).then_inc(const_step, 1)
            pool.memset(lower[:, :], 1.0).then_inc(const_step, 1)
            pool.memset(ident[:, :], 0.0).then_inc(const_step, 1)
            pool.wait_ge(const_step, 3)
            carry3 = carry[:, :].rearrange("p (e t) -> p e t", t=T)
            pool.affine_select(carry3, carry3, pattern=[[0, E], [1, T]], compare_op=ALU.is_gt, fill=0.0,
                               base=0, channel_multiplier=0).then_inc(consts, 1)
            pool.affine_select(lower[:, :], lower[:, :], pattern=[[1, P]], compare_op=ALU.is_gt, fill=0.0,
                               base=0, channel_multiplier=-1).then_inc(consts, 1)
            pool.affine_select(ident[:, :], ident[:, :], pattern=[[-1, P]], compare_op=ALU.not_equal, fill=1.0,
                               base=0, channel_multiplier=1).then_inc(consts, 1)
            last_slot, zero_row = pool.to_reg(NSLOT - 1), pool.to_reg(NSLOT)

            def step_a(t, u):
                own_wait()
                pool.wait_ge(h_ready, t + 2)
                pool.tensor_tensor(xs[:, at(t)], xs[:, at(t)], h[:, 1 - u, :], ALU.add).then_inc(x1_ready, 1)
                own_wait()
                pool.wait_ge(x1_ready, t + 1)
                wait_past(pool, xk_ready, t - 1)
                pool.tensor_tensor(dx[:, u, :], xs[:, at(t - 1)], xs[:, at(t)], ALU.subtract).then_inc(dx_ready, 1)

            def scatter(t, u, sent):
                wait_past(pool, scat[u], sent * 16)
                pool.tensor_copy(idx[:, u:u + 1], slot_i[:, bass.ds(t, 1)]).then_inc(idx_ready, 1)
                pool.wait_ge(idx_ready, t + 1)
                pool.wait_ge(row_ready, t + 1)
                pool.sem_inc(pool_paced, 1)
                pool.indirect_dma_start(rows, bass.IndirectOffsetOnAxis(idx[:, u:u + 1], axis=0), row[:, u, :], None,
                                        bounds_check=last_slot, oob_is_err=False).then_inc(scat[u], 16)

            step_a(0, 0)
            step_a(1, 1)
            pool.wait_ge(slots_ready, 1)
            pool.wait_ge(zfill, 16 * (ZPARTS + 1))
            scatter(0, 0, 0)
            step_a(2, 0)
            scatter(1, 1, 0)
            step_a(3, 1)
            scatter(2, 0, 1)
            with pool.Fori(2, NP) as n:
                step_a(2 * n, 0)
                scatter(2 * n - 1, 1, n - 1)
                step_a(2 * n + 1, 1)
                scatter(2 * n, 0, n)
            scatter(T - 1, 1, NP - 1)

            def deltas(n):
                wait_past(pool, xr_ready, n)
                own_wait()
                pool.tensor_tensor(dx2[:, :], xs[:, pair(n, before=1)], xs[:, pair(n)], ALU.subtract)\
                    .then_inc(dx2_ready, 1)

            for n in range(EARLY + 1):
                deltas(n)

            def split_weights(e, u, n):
                pool.wait_ge(kv_in[u], (n + 1) * 32)
                wait_past(pool, o_mm, e - 1)
                for j, wide in enumerate((wkr, wvr)):
                    part = [wide[:, u, c, :, :].rearrange("p a b -> p (a b)") for c in (HI, LO)]
                    pool.sem_inc(pool_paced, 1)
                    pool.tensor_copy(part[HI], wkv[:, u, j, :]).then_inc(w_hi, 1)
                    pool.wait_ge(w_hi, e * 2 + j + 1)
                    pool.tensor_tensor(part[LO], wkv[:, u, j, :], part[HI].bitcast(F32), ALU.subtract).then_inc(w_lo, 1)

            pool.wait_ge(w_lo, 2)
            split_weights(1, 1, 0)
            with pool.Fori(1, E // 2) as i:
                split_weights(2 * i, 0, i)
                split_weights(2 * i + 1, 1, i)

            def gather(n, q, s, done):
                t, u = 2 * n + s, 2 * q + s
                wait_past(pool, gath[u], done * 16)
                wait_past(pool, yT_mm, n - 1)
                pool.tensor_copy(idx[:, u:u + 1], slot_i[:, bass.ds(t, 1)]).then_inc(idy_ready, 1)
                pool.wait_ge(idy_ready, t + 1)
                pool.sem_inc(pool_paced, 1)
                pool.indirect_dma_start(yrow[:, u, :], None, yrows, bass.IndirectOffsetOnAxis(idx[:, u:u + 1], axis=0),
                                        bounds_check=zero_row, oob_is_err=False).then_inc(gath[u], 16)

            def add_y(n, q):
                pool.wait_ge(ry_ready, n + 1)
                if exists(n + 1):
                    pool.wait_ge(dx2_ready, n + 2)
                pool.sem_inc(pool_paced, 1)
                pool.tensor_tensor(xs[:, pair(n)], xs[:, pair(n)], rr[:, q, :], ALU.add).then_inc(x2_ready, 1)

            def add_h3(n, q):
                own_wait()
                pool.wait_ge(h3_ready, 2 * n + 3)
                pool.tensor_tensor(xs[:, pair(n)], xs[:, pair(n)],
                                   h3[:, 2 * q:2 * q + 2, :].rearrange("p s w -> p (s w)"), ALU.add)\
                    .then_inc(out_ready, 1)

            def pair_c(n, q, i):
                if exists(n + 4, start=EARLY + 1):
                    deltas(n + 4)
                if exists(n + 2):
                    add_y(n + 2, q)
                if exists(n + 4):
                    for s in range(2):
                        gather(n + 4, q, s, i + 2)
                if exists(n - 2):
                    add_h3(n - 2, q)

            pool.wait_ge(y_out[0], 16 * (E // 2))
            pool.wait_ge(y_out[1], 16 * (E // 2))
            for n in range(-AHEAD, 4):
                pair_c(n, n % 2, n // 2)
            with pool.Fori(2, NP // 2 - 2) as i:
                pair_c(2 * i, 0, i)
                pair_c(2 * i + 1, 1, i)
            for n in range(NP - AHEAD, NP + 2):
                pair_c(n, n % 2, n // 2)


def _halves(a):
    return a.reshape(K, P, -1).transpose(1, 0, 2)


def kernel(x, cond_1024, itok_BxS_2_50255, L0_cond_W_z, L0_cond_U_z, L0_cond_C_z, L0_cond_b_z, L0_cond_W_r,
           L0_cond_U_r, L0_cond_C_r, L0_cond_b_r, L0_cond_W, L0_cond_U, L0_cond_C, L0_cond_b,
           L1_cond_time_maa_k, L1_cond_time_maa_r, L1_cond_w_recept, L1_cond_w_key, L1_cond_w_value,
           L2_cond_W, L2_cond_b, L2_cond_alpha, L3_cond_Wx, L3_cond_Wh, L3_cond_b):
    import concourse.bacc as bacc
    from concourse.bass_utils import run_bass_kernel_spmd

    a = np.asarray
    l2 = a(L2_cond_W).T
    cmats = [L0_cond_C_r, L0_cond_C_z, L0_cond_C]
    mats = [L0_cond_U_r, L0_cond_U_z, L0_cond_U, l2[:D], L3_cond_Wh]
    smats = [L0_cond_W_r, L0_cond_W_z, L0_cond_W, a(L1_cond_w_recept).T, l2[D:], L3_cond_Wx]
    vecs = [L0_cond_b_z, L0_cond_b_r, L0_cond_b, L1_cond_time_maa_k, L1_cond_time_maa_r, L2_cond_b, L2_cond_alpha,
            L3_cond_b]
    laid = {
        "x": a(x).reshape(B, T, K, P).transpose(3, 1, 2, 0).reshape(P, T * W),
        "cond": a(cond_1024).reshape(B, K, P).transpose(2, 1, 0).reshape(P, W),
        "ids": a(itok_BxS_2_50255),
        "cmats": np.stack([_halves(a(m)) for m in cmats], 1),
        "mats": np.stack([_halves(a(m)) for m in mats], 1),
        "smats": np.stack([_halves(a(m)) for m in smats], 1),
        "vecs": np.stack([a(v).reshape(K, P).T for v in vecs], 1),
        "w_key": a(L1_cond_w_key).reshape(E, K, P, F).transpose(2, 0, 1, 3).reshape(P, E * K * F),
        "w_value": a(L1_cond_w_value).reshape(E, FT, P, D).transpose(2, 0, 1, 3).reshape(P, E * FT * D),
    }
    laid = {n: np.ascontiguousarray(v) for n, v in laid.items()}

    nc = bacc.Bacc("TRN2", target_bir_lowering=False, num_devices=1)
    args = [nc.dram_tensor(n, v.shape, mybir.dt.from_np(v.dtype), kind="ExternalInput").ap() for n, v in laid.items()]
    out = nc.dram_tensor("out", (P, T * W), F32, kind="ExternalOutput").ap()
    rows = nc.dram_tensor("rows", (NSLOT, D), F32, kind="Internal").ap()
    yrows = nc.dram_tensor("yrows", (NSLOT + 1, D), F32, kind="Internal").ap()
    build(nc, *args, out, rows, yrows)
    r = run_bass_kernel_spmd(nc, [laid], core_ids=[0])
    got = r.results[0]["out"]
    return got.reshape(P, T, K, B).transpose(3, 1, 2, 0).reshape(B, T, D)
```

```python
import numpy as np
from contextlib import ExitStack

import concourse.bass as bass
import concourse.mybir as mybir

F32 = mybir.dt.float32
F32R = mybir.dt.float32r
I32 = mybir.dt.int32
ALU = mybir.AluOpType
ACT = mybir.ActivationFunctionType
AX = mybir.AxisListType

P = 128
B, T, D = 128, 64, 256
K = D // P
W = K * B
NP = T // 2
E, F = 16, 512
C = B * T // E
FT = F // P
ST = C // P
NSLOT = E * C
HASH = 5099 % E
NVEC = 8
V_BZ, V_BR, V_BH, V_MK, V_MR, V_B2, V_AL, V_B3 = range(NVEC)
C_R, C_Z, C_H = range(3)
U_R, U_Z, U_H, L2_H, L3_H = range(5)
S_R, S_Z, S_H, S_REC, S_L2, S_L3 = range(6)
HI, LO = 0, 1
AHEAD = 4
EARLY = 4
RA = 10


def wait_past(eng, sem, count):
    if not isinstance(count, int) or count > 0:
        eng.wait_ge(sem, count)


def exists(m, end=NP, start=0):
    return not isinstance(m, int) or start <= m < end


def build(nc, x, cond, ids, cmats, mats, smats, vecs, w_key, w_value, out, rows, yrows):
    with ExitStack() as ctx:
        scope = [ctx]

        def sb(name, shape, dt=F32):
            return scope[0].enter_context(nc.sbuf_tensor(name, shape, dt))

        def sem(name):
            return ctx.enter_context(nc.semaphore(name))

        bank = [ctx.enter_context(nc.psum_tensor(f"bank{i}", [P, 512], F32)) for i in range(8)]

        def pair_of(bk):
            return bk[:, :].rearrange("p (o s b) -> p o s b", o=K, s=2)

        xs = sb("xs", [P, (T + 1) * W])
        wm = sb("wm", [P, 5, K, D])
        wr = sb("wr", [P, 6, 2, K, D], F32R)
        vec = sb("vec", [P, NVEC, K])
        ident = sb("ident", [P, P])
        slot_i = sb("slot_i", [P, T], I32)
        idx = sb("idx", [P, 4], I32)

        rr = sb("rr", [P, EARLY, 2 * W])
        dx2 = [sb("dx2", [P, 2 * W])]
        xr = [sb("xr", [P, 2 * W])]
        xrs = [sb("xrs", [P, 2, 2, K, B], F32R)]

        phases = ctx.enter_context(ExitStack())
        scope[0] = phases
        wkv = sb("wkv", [P, 2, 2, K * F])
        ein = sb("ein", [P, ST, D])

        with ExitStack() as phase:
            scope[0] = phase
            wc = sb("wc", [P, 3, K, D])
            zeros = sb("zeros", [P, D])
            warm = sb("warm", [P, 1])
            onehot = sb("onehot", [P, E, T])
            eidx = sb("eidx", [P, E, T])
            carry = sb("carry", [P, E * T])
            count = sb("count", [P, E * T])
            total, before = sb("total", [P, E]), sb("before", [P, E])
            lower = sb("lower", [P, P])
            id_i = sb("id_i", [P, T], I32)
            ef, pos, keep, slot_f = (sb(n, [P, T]) for n in ("ef", "pos", "keep", "slot_f"))
        scope[0] = phases
        wkr = sb("wkr", [P, 2, 2, K, F], F32R)
        wvr = sb("wvr", [P, 2, 2, FT, D], F32R)

        with ExitStack() as phase:
            scope[0] = phase
            wsrc = sb("wsrc", [P, 6, K, D])
            v2 = sb("v2", [P, 3, K, 2, B])
            xsp = sb("xsp", [P, 2, 2, 2, K, B], F32R)
            h = sb("h", [P, 2, W])
            rg = sb("rg", [P, K, B])
            zg = sb("zg", [P, K, B])
            hh = sb("hh", [P, K, B])
            wh = sb("wh", [P, W])
            dx = sb("dx", [P, 2, W])
            xk = sb("xk", [P, W])
            row = sb("row", [P, 4, D])
        with ExitStack() as phase:
            scope[0] = phase
            einr = sb("einr", [P, 2, K, C], F32R)
            hrel = sb("hrel", [P, 2, C])
            hsq = sb("hsq", [P, 2, C])
            hidr = sb("hidr", [P, 2, FT, C], F32R)
            yo = sb("yo", [P, 2, ST, D])
        phases.close()
        with ExitStack() as phase:
            scope[0] = phase
            dx2.append(sb("dx2_even", [P, 2 * W]))
            xr.append(sb("xr_even", [P, 2 * W]))
            xrs.append(sb("xrs_odd", [P, 2, 2, K, B], F32R))
            rr_on = sb("rr_on", [P, (NP - EARLY) * 2 * W])
            yrow = sb("yrow", [P, 4, D])
            x2s = sb("x2s", [P, 2, 2, K, B], F32R)
            x3s = sb("x3s", [P, 2, 2, K, B], F32R)
            h2 = sb("h2", [P, 2, W])
            h3 = sb("h3", [P, 4, W])
            leak_t = sb("leak_t", [P, W])
            g2 = sb("g2", [P, W])
            gz, pre, hl = sb("gz", [P, W]), sb("pre", [P, W]), sb("hl", [P, W])

        x0_in, x_in, c_in, id_in = sem("x0_in"), sem("x_in"), sem("c_in"), sem("id_in")
        cm_in = [sem(f"cm_in_{g}") for g in "rzh"]
        um_in, ws_in, wrest_in = sem("um_in"), sem("ws_in"), sem("wrest_in")
        zfill, zeros_set = sem("zfill"), sem("zeros_set")
        consts, const_step, warmed = sem("consts"), sem("const_step"), sem("warmed")
        leak_ready = sem("leak_ready")
        route_step = sem("route_step")
        total_ready, before_mm, slots_ready = sem("total_ready"), sem("before_mm"), sem("slots_ready")
        v_mm, v_ready = sem("v_mm"), sem("v_ready")
        ws_hi, ws_lo = sem("ws_hi"), sem("ws_lo")
        x_hi, x_lo = sem("x_hi"), sem("x_lo")
        h_ready = sem("h_ready")
        proj_mm = [sem(f"proj_mm_{g}") for g in "rzh"]
        cond_in = [sem(f"cond_in_{g}") for g in "rzh"]
        r_mm, z_mm, c_mm = sem("r_mm"), sem("z_mm"), sem("c_mm")
        r_sig, z_sig, c_tanh = sem("r_sig"), sem("z_sig"), sem("c_tanh")
        rh_ready, wh_ready, ph_ready = sem("rh_ready"), sem("wh_ready"), sem("ph_ready")
        x1_ready, dx_ready, xk_ready = sem("x1_ready"), sem("dx_ready"), sem("xk_ready")
        tr_mm, row_ready, idx_ready = sem("tr_mm"), sem("row_ready"), sem("idx_ready")
        scat = [sem(f"scat{i}") for i in range(4)]
        kv_in = [sem("kv_in0"), sem("kv_in1")]
        ein_in = [sem("ein_in0"), sem("ein_in1")]
        key_hi, value_hi, w_lo = sem("key_hi"), sem("value_hi"), sem("w_lo")
        einT_mm, ein_hi, ein_lo = sem("einT_mm"), sem("ein_hi"), sem("ein_lo")
        h_mm, rel_ready, sq_ready = sem("h_mm"), sem("rel_ready"), sem("sq_ready")
        hid_hi, hid_lo = sem("hid_hi"), sem("hid_lo")
        o_mm, o_ready = sem("o_mm"), sem("o_ready")
        y_out = [sem("y_out0"), sem("y_out1")]
        idy_ready = sem("idy_ready")
        gath = [sem(f"gath{i}") for i in range(4)]
        dx2_ready, xr_ready, xr_hi, xr_lo = sem("dx2_ready"), sem("xr_ready"), sem("xr_hi"), sem("xr_lo")
        rec_mm, rec_sig, yT_mm, ry_ready = sem("rec_mm"), sem("rec_sig"), sem("yT_mm"), sem("ry_ready")
        x2_ready, x2_hi, x2_lo = sem("x2_ready"), sem("x2_hi"), sem("x2_lo")
        x3_ready, x3_hi, x3_lo = sem("x3_ready"), sem("x3_hi"), sem("x3_lo")
        x2_used, x3_used = sem("x2_used"), sem("x3_used")
        h2_ready, h3_ready, hl_ready = sem("h2_ready"), sem("h3_ready"), sem("hl_ready")
        g_mm, g_sig, gz_ready, pre_ready = sem("g_mm"), sem("g_sig"), sem("gz_ready"), sem("pre_ready")
        p3_mm, out_ready, stored = sem("p3_mm"), sem("out_ready"), sem("stored")
        pool_paced = sem("pool_paced")

        FIRST = 4

        def loads_of(n):
            if isinstance(n, int) and n < FIRST:
                return 16
            return (n - (FIRST - 2)) * 16
        ZPARTS = 4
        ZR = NSLOT // ZPARTS

        def at(t):
            return bass.ds(t * W + W, W)

        def pair(n, before=0):
            return bass.ds(n * 2 * W + (1 - before) * W, 2 * W)

        def half(k):
            return slice(k * B, (k + 1) * B)

        def split_of(tile):
            return lambda c, k: tile[:, c, :, k, :]

        def parity(q):
            return (q + RA) % 2

        def rr_of(n):
            if isinstance(n, int) and n < EARLY:
                return rr[:, n, :]
            return rr_on[:, bass.ds((n - EARLY) * 2 * W, 2 * W)]

        def over_pairs(eng, pair_c):
            for n in range(-AHEAD, 4):
                pair_c(n, n % 2, n // 2, True)
            full = (NP - RA - 1) // 2
            with eng.Fori(2, full) as i:
                pair_c(2 * i, 0, i, True)
                pair_c(2 * i + 1, 1, i, True)
            for n in range(2 * full, 2 * full + 2):
                pair_c(n, n % 2, n // 2, True)
            with eng.Fori(full + 1, NP // 2 - 2) as i:
                pair_c(2 * i, 0, i, False)
                pair_c(2 * i + 1, 1, i, False)
            for n in range(NP - AHEAD, NP + 2):
                pair_c(n, n % 2, n // 2, True)

        block = ctx.enter_context(nc.Block())

        @block.sync
        def _(sp):
            sp.dma_start(xs[:, 0:W], cond).then_inc(c_in, 16)
            sp.dma_start(vec[:, :, :], vecs).then_inc(c_in, 16)
            sp.dma_start(xs[:, pair(0)], x[:, 0:2 * W]).then_inc(x0_in, 16)
            sp.dma_start(wsrc[:, 0:3, :, :], smats[:, 0:3, :, :]).then_inc(ws_in, 16)
            sp.dma_start(wm[:, U_R:U_H + 1, :, :], mats[:, U_R:U_H + 1, :, :]).then_inc(um_in, 16)
            sp.dma_start(xs[:, W + 2 * W:W + FIRST * 2 * W], x[:, 2 * W:FIRST * 2 * W]).then_inc(x_in, 16)
            sp.wait_ge(zeros_set, 1)
            for i in range(ZPARTS):
                sp.dma_start(rows[i * ZR:(i + 1) * ZR, :].rearrange("(p s) d -> p s d", p=P),
                             zeros[:, :].unsqueeze(1).broadcast_to([P, ZR // P, D])).then_inc(zfill, 16)
            sp.dma_start(yrows[NSLOT:NSLOT + 1, :], zeros[0:1, :]).then_inc(zfill, 16)
            with sp.Fori(FIRST, NP) as n:
                sp.wait_ge(x_in, loads_of(n) - 16)
                sp.dma_start(xs[:, pair(n)], x[:, bass.ds(n * 2 * W, 2 * W)]).then_inc(x_in, 16)

            sp.dma_start(wsrc[:, 3:6, :, :], smats[:, 3:6, :, :]).then_inc(wrest_in, 16)
            sp.dma_start(wm[:, L2_H:L3_H + 1, :, :], mats[:, L2_H:L3_H + 1, :, :]).then_inc(wrest_in, 16)

            def load_kv(e, u):
                sp.dma_start(wkv[:, u, 0, :], w_key[:, bass.ds(e * K * F, K * F)]).then_inc(kv_in[u], 16)
                sp.dma_start(wkv[:, u, 1, :], w_value[:, bass.ds(e * FT * D, FT * D)]).then_inc(kv_in[u], 16)

            def load_rows(e, u):
                sp.dma_start(ein[:, :, :],
                             rows[bass.ds(e * C, C), :].rearrange("(s p) d -> p s d", p=P)).then_inc(ein_in[u], 16)

            def store(e, u):
                sp.wait_ge(o_ready, (e + 1) * 2)
                sp.dma_start(yrows[bass.ds(e * C, C), :].rearrange("(s p) d -> p s d", p=P),
                             yo[:, u, :, :]).then_inc(y_out[u], 16)

            load_kv(0, 0)
            load_kv(1, 1)
            for u in range(4):
                sp.wait_ge(scat[u], 16 * (T // 4))
            load_rows(0, 0)
            sp.wait_ge(einT_mm, K)
            load_rows(1, 1)
            with sp.Fori(1, E // 2) as n:
                for u in range(2):
                    sp.wait_ge(w_lo, (2 * n + u - 1) * 2)
                    load_kv(2 * n + u, u)
                    sp.wait_ge(einT_mm, (2 * n + u) * K)
                    load_rows(2 * n + u, u)
                    store(2 * n + u - 2, u)
            for e in range(E - 2, E):
                store(e, e % 2)
            with sp.Fori(0, NP) as n:
                sp.wait_ge(out_ready, n + 1)
                sp.dma_start(out[:, bass.ds(n * 2 * W, 2 * W)], xs[:, pair(n)]).then_inc(stored, 16)
            sp.wait_ge(stored, 16 * NP)

        @block.tensor
        def _(pe):
            gates = [bank[0:2], bank[2:4], bank[4:6]]
            MISC, TR = bank[6], bank[7]

            def prod32(dst, w, rhs, start=False, ready=None):
                for k in range(K):
                    if ready:
                        pe.wait_ge(ready[0], ready[1] + k + 1)
                    for o in range(K):
                        mm = pe.matmul(dst(o), w[:, k, o * P:(o + 1) * P], rhs(k),
                                       start=start and o == 0 and k == 0, stop=k == K - 1, skip_group_check=True)
                return mm

            def receptance(n, p, bk, banks):
                pe.wait_ge(xr_lo, n + 1)
                wait_past(pe, rec_sig, n + 1 - banks)
                prod_split(bk, S_REC, split_of(xrs[p])).then_inc(rec_mm, 1)

            def prod_split(bk, m, rhs, first=0, last=6 * K):
                passes = [(o, k, a, b) for o in range(K) for k in range(K) for a, b in ((HI, HI), (HI, LO), (LO, HI))]
                for o, k, a, b in passes[first:last]:
                    mm = pe.matmul(pair_of(bk)[:, o, :, :], wr[:, m, a, k, o * P:(o + 1) * P], rhs(b, k),
                                   start=(o, k, a, b) == (0, 0, HI, HI), stop=False, skip_group_check=True)
                return mm

            def step_of(bk, s):
                return lambda o: pair_of(bk)[:, o, s, :]

            def keep_warm(count, w, bk=5):
                for _ in range(count):
                    pe.matmul(bank[bk][:, 0:P], w[:, 0:P], w[:, 0:P], start=True, stop=True)

            pe.wait_ge(zeros_set, 1)
            keep_warm(9, zeros)

            pe.wait_ge(c_in, 32)
            for g, m in enumerate((C_R, C_Z, C_H)):
                pe.wait_ge(cm_in[m], 16)
                prod32(lambda o: gates[g][1][:, half(o)], wc[:, m, :, :], lambda k: xs[:, half(k)], True)\
                    .then_inc(v_mm, 1)
                if g == 0:
                    pe.wait_ge(consts, 4)
                    pe.wait_ge(total_ready, 1)
                    pe.matmul(MISC[:, 0:E], lower[:, :], total[:, :], start=True, stop=True).then_inc(before_mm, 1)

            def turn_rows(t):
                pe.wait_ge(xk_ready, t + 1)
                wait_past(pe, row_ready, t)
                for k in range(K):
                    mm = pe.transpose(TR[:, k * P:(k + 1) * P], xk[:, half(k)], ident[:, :])
                mm.then_inc(tr_mm, 1)

            def pair_a(n, q):
                xn = split_of(xsp[:, 1 - q, :, :, :, :])
                for s in range(2):
                    t = 2 * n + s
                    more = exists(n + 1)
                    for g, (m, done) in enumerate(((U_R, r_mm), (U_Z, z_mm), (U_H, c_mm))):
                        if s == 0:
                            pe.wait_ge(cond_in[g], n + 1)
                        if g == 2:
                            if more and s == 0:
                                pe.wait_ge(x_lo, n + 2)
                                prod_split(gates[0][1 - q], S_R, xn, 0, 4)
                            if more and s == 1:
                                prod_split(gates[1][1 - q], S_Z, xn, 6, 10)
                        rhs = (lambda k: rg[:, k, :]) if g == 2 else (lambda k: h[:, s, half(k)])
                        prod32(step_of(gates[g][q], s), wm[:, m, :, :], rhs,
                               ready=(rh_ready if g == 2 else h_ready, 2 * t)).then_inc(done, 1)
                    if more and s == 0:
                        prod_split(gates[0][1 - q], S_R, xn, 4).then_inc(proj_mm[0], 1)
                        prod_split(gates[1][1 - q], S_Z, xn, 0, 6)
                    if more and s == 1:
                        prod_split(gates[1][1 - q], S_Z, xn, 10).then_inc(proj_mm[1], 1)
                        prod_split(gates[2][1 - q], S_H, xn).then_inc(proj_mm[2], 1)
                    if isinstance(t, int) and t == T - 2:
                        receptance(0, 0, MISC, 1)
                    if exists(t - 1, end=T):
                        turn_rows(t - 1)
                    if isinstance(t, int) and t == T - 1:
                        receptance(1, 0, MISC, 1)

            pe.wait_ge(x_lo, 1)
            for g, m in enumerate((S_R, S_Z, S_H)):
                pe.wait_ge(ws_lo, g + 1)
                prod_split(gates[g][0], m, split_of(xsp[:, 0, :, :, :, :])).then_inc(proj_mm[g], 1)
            pe.wait_ge(um_in, 16)
            pe.wait_ge(v_ready, 3)
            pair_a(0, 0)
            pair_a(1, 1)
            with pe.Fori(1, NP // 2 - 1) as i:
                pair_a(2 * i, 0)
                pair_a(2 * i + 1, 1)
            pair_a(NP - 2, 0)
            pair_a(NP - 1, 1)
            turn_rows(T - 1)

            TT, HB, OB = bank[0:2], bank[2:4], bank[4:8]

            def turn_in(e, u, n):
                pe.wait_ge(ein_in[u], (n + 1) * 16)
                wait_past(pe, ein_lo, e * K)
                for k in range(K):
                    for s in range(ST):
                        mm = pe.transpose(TT[k][:, s * P:(s + 1) * P], ein[:, s, k * P:(k + 1) * P], ident[:, :])
                    mm.then_inc(einT_mm, 1)

            def hidden(e, u):
                pe.wait_ge(w_lo, e * 2 + 1)
                for f in range(FT):
                    wait_past(pe, rel_ready, e * FT + f - 1)
                    for k in range(K):
                        if f == 0:
                            pe.wait_ge(ein_lo, e * K + k + 1)
                        for a, b in ((HI, HI), (HI, LO), (LO, HI)):
                            mm = pe.matmul(HB[f % 2][:, :], wkr[:, u, a, k, f * P:(f + 1) * P], einr[:, b, k, :],
                                           start=k == 0 and (a, b) == (HI, HI), stop=k == K - 1 and a == LO)
                    mm.then_inc(h_mm, 1)

            def project(e, u):
                pe.wait_ge(w_lo, (e + 1) * 2)
                wait_past(pe, o_ready, (e - 1) * 2)
                for f in range(FT):
                    pe.wait_ge(hid_lo, e * FT + f + 1)
                    for s in range(ST):
                        for a, b in ((HI, HI), (HI, LO), (LO, HI)):
                            mm = pe.matmul(OB[2 * u + s // 2][:, (s % 2) * D:(s % 2 + 1) * D],
                                           hidr[:, a, f, s * P:(s + 1) * P], wvr[:, u, b, f, :],
                                           start=f == 0 and s % 2 == 0 and (a, b) == (HI, HI),
                                           stop=f == FT - 1 and a == LO, skip_group_check=True)
                mm.then_inc(o_mm, 1)

            def experts(i, last=False):
                for u in range(2):
                    hidden(2 * i + u, u)
                    if not (last and u):
                        turn_in(2 * i + u + 1, 1 - u, i + u)
                    project(2 * i + u, u)

            for n in range(2, EARLY):
                receptance(n, 0, MISC, 1)
            turn_in(0, 0, 0)
            pe.wait_ge(rec_sig, EARLY)
            experts(0)
            with pe.Fori(1, E // 2 - 1) as i:
                experts(i)
            experts(E // 2 - 1, last=True)

            G, Q, REC, Y = bank[0:2], bank[2:4], bank[4:6], bank[6:8]

            def turn_y(n, q, s, count):
                if s == 0:
                    wait_past(pe, ry_ready, n - 1)
                pe.wait_ge(gath[2 * q + s], count * 16)
                for k in range(K):
                    mm = pe.transpose(Y[q][:, s * W + k * B:s * W + (k + 1) * B],
                                      yrow[:, 2 * q + s, k * P:(k + 1) * P], ident[:, :])
                mm.then_inc(yT_mm, 1)

            def proj2(n, q):
                pe.wait_ge(x2_lo, n + 1)
                prod_split(G[q], S_L2, split_of(x2s)).then_inc(x2_used, 1)

            def proj3(n, q):
                pe.wait_ge(x3_lo, n + 1)
                prod_split(Q[q], S_L3, split_of(x3s)).then_inc(x3_used, 1)

            def step3(t, q, s):
                pe.wait_ge(h3_ready, t + 1)
                prod32(step_of(Q[q], s), wm[:, L3_H, :, :], lambda k: h3[:, (2 * q + s - 1) % 4, half(k)])\
                    .then_inc(p3_mm, 1)

            def step2(t, q, s):
                prod32(step_of(G[q], s), wm[:, L2_H, :, :], lambda k: h2[:, 1 - s, half(k)],
                       ready=(h2_ready, 2 * t)).then_inc(g_mm, 1)

            def pair_c(n, q, i, ahead):
                if isinstance(n, int) and n in (-2, -1):
                    keep_warm(3, ident, 0)
                full = ahead and exists(n + RA)
                if exists(n):
                    step2(2 * n, q, 0)
                if exists(n + 1):
                    proj2(n + 1, 1 - q)
                if exists(n + 3):
                    turn_y(n + 3, 1 - q, 0, i + 2 + q)
                    if full:
                        turn_y(n + 3, 1 - q, 1, i + 2 + q)
                if exists(n - 2):
                    step3(2 * n - 3, q, 1)
                if exists(n):
                    step2(2 * n + 1, q, 1)
                if exists(n - 1):
                    proj3(n - 1, 1 - q)
                if exists(n + 3) and not full:
                    turn_y(n + 3, 1 - q, 1, i + 2 + q)
                if ahead and exists(n + RA, start=RA):
                    receptance(n + RA, parity(q), REC[parity(q)], 2)
                if exists(n - 1):
                    step3(2 * n - 2, 1 - q, 0)

            pe.wait_ge(o_ready, (E - 1) * 2)
            for n in range(EARLY, RA):
                receptance(n, n % 2, REC[n % 2], 2)
            pe.wait_ge(o_ready, E * 2)
            over_pairs(pe, pair_c)

        @block.scalar
        def _(act):
            def own_wait():
                act.wait_ge(zeros_set, 1)

            act.dma_start(id_i[:, :], ids).then_inc(id_in, 16)
            for m in (C_R, C_Z, C_H):
                act.dma_start(wc[:, m, :, :], cmats[:, m, :, :]).then_inc(cm_in[m], 16)
            act.wait_ge(zeros_set, 1)
            act.activation(warm[:, :], zeros[:, 0:1], ACT.Sigmoid).then_inc(warmed, 1)

            gates = [bank[0:2], bank[2:4], bank[4:6]]
            MISC, TR = bank[6], bank[7]

            def split_matrix(m):
                act.activation(wr[:, m, HI, :, :], wsrc[:, m, :, :], ACT.Copy).then_inc(ws_hi, 1)

            def split_x(n, q):
                own_wait()
                if isinstance(n, int) and n == 0:
                    act.wait_ge(x0_in, 16)
                else:
                    act.wait_ge(x_in, loads_of(n))
                wait_past(act, proj_mm[2], n - 1)
                act.activation(xsp[:, q, HI, :, :, :].rearrange("p s k b -> p (s k b)"),
                               xs[:, pair(n)], ACT.Copy).then_inc(x_hi, 1)

            def row_out(t, u, sent):
                act.wait_ge(tr_mm, t + 1)
                wait_past(act, scat[u], sent * 16)
                act.activation(row[:, u, :], TR[:, 0:D], ACT.Copy).then_inc(row_ready, 1)

            def high_key(e, u, n):
                act.wait_ge(kv_in[u], (n + 1) * 32)
                wait_past(act, h_mm, (e - 1) * FT)
                act.activation(wkr[:, u, HI, :, :].rearrange("p a b -> p (a b)"), wkv[:, u, 0, :], ACT.Copy)\
                   .then_inc(key_hi, 1)

            def high_xr(n, src, p, bufs):
                act.wait_ge(xr_ready, n + 1)
                wait_past(act, rec_mm, n + 1 - bufs)
                act.activation(xrs[p][:, HI, :, :, :].rearrange("p s k b -> p (s k b)"), xr[src][:, :], ACT.Copy)\
                   .then_inc(xr_hi, 1)

            def receptance(n, bk):
                own_wait()
                act.wait_ge(rec_mm, n + 1)
                act.activation(rr_of(n).rearrange("p (s k b) -> p k s b", s=2, k=K), pair_of(bk), ACT.Sigmoid)\
                   .then_inc(rec_sig, 1)

            def spare(t):
                if t == T - 8:
                    act.wait_ge(wrest_in, 32)
                if T - 8 <= t < T - 5:
                    split_matrix(3 + t - (T - 8))
                if t == T - 5:
                    act.wait_ge(slots_ready, 1)
                    act.wait_ge(zfill, 16 * (ZPARTS + 1))
                    high_key(0, 0, 0)
                if t == T - 4:
                    high_xr(0, 0, 0, 1)
                if t == T - 3:
                    act.activation(wvr[:, 0, HI, :, :].rearrange("p a b -> p (a b)"), wkv[:, 0, 1, :], ACT.Copy)\
                       .then_inc(value_hi, 1)
                if t == T - 2:
                    receptance(0, MISC)
                    high_xr(1, 0, 0, 1)

            def pair_a(n, q, i):
                for s in range(2):
                    t = 2 * n + s
                    for g, (dst, f, mm, done) in enumerate(((rg, ACT.Sigmoid, r_mm, r_sig),
                                                            (zg, ACT.Sigmoid, z_mm, z_sig),
                                                            (hh, ACT.Tanh, c_mm, c_tanh))):
                        act.wait_ge(mm, t + 1)
                        act.activation(dst[:, :, :], pair_of(gates[g][q])[:, :, s, :], f).then_inc(done, 1)
                        if g == 1 and s == 0 and exists(n + 2):
                            split_x(n + 2, q)
                    if exists(t - 1, end=T):
                        row_out(t - 1, (2 * q + s - 1) % 4, i - 1 if q == s == 0 else i)
                    if isinstance(t, int):
                        spare(t)

            split_x(0, 0)
            act.wait_ge(ws_in, 16)
            for m in range(3):
                split_matrix(m)
            act.wait_ge(c_in, 32)
            for g, v in enumerate((V_BR, V_BZ, V_BH)):
                act.wait_ge(v_mm, g + 1)
                for k in range(K):
                    a = act.activation(v2[:, g, k, :, :],
                                       gates[g][1][:, half(k)].unsqueeze(1).broadcast_to([P, 2, B]),
                                       ACT.Identity, bias=vec[:, v, k:k + 1])
                a.then_inc(v_ready, 1)
            split_x(1, 1)

            for n in range(4):
                pair_a(n, n % 2, n // 2)
            with act.Fori(2, NP // 2 - 2) as i:
                pair_a(2 * i, 0, i)
                pair_a(2 * i + 1, 1, i)
            for n in range(NP - 4, NP):
                pair_a(n, n % 2, n // 2)
            receptance(1, MISC)
            row_out(T - 1, 3, T // 4 - 1)
            for n in range(2, EARLY):
                high_xr(n, 0, 0, 1)
                if n == 2:
                    high_key(1, 1, 0)
                receptance(n, MISC)

            TT, HB, OB = bank[0:2], bank[2:4], bank[4:8]

            def split_in(e):
                for k in range(K):
                    act.wait_ge(einT_mm, e * K + k + 1)
                    if k == 0:
                        wait_past(act, h_mm, e * FT)
                    act.activation(einr[:, HI, k, :], TT[k][:, :], ACT.Copy).then_inc(ein_hi, 1)

            def high_sq(e, f):
                act.wait_ge(sq_ready, e * FT + f + 1)
                act.activation(hidr[:, HI, f, :], hsq[:, f % 2, :], ACT.Copy).then_inc(hid_hi, 1)

            def expert(e, u, sent, ahead, last=False):
                for f in range(FT):
                    act.wait_ge(h_mm, e * FT + f + 1)
                    wait_past(act, sq_ready, e * FT + f - 1)
                    act.activation(hrel[:, f % 2, :], HB[f % 2][:, :], ACT.Relu).then_inc(rel_ready, 1)
                    if f > 0:
                        high_sq(e, f - 1)
                high_sq(e, FT - 1)
                if not last:
                    split_in(e + 1)
                if isinstance(e, int) and e == 0:
                    high_xr(EARLY, 0, 0, 1)
                if ahead is not None:
                    high_key(e + 2, u, ahead)
                if last:
                    act.wait_ge(w_lo, 2 * E)
                    high_xr(EARLY + 1, 0, 1, 2)
                act.wait_ge(o_mm, e + 1)
                wait_past(act, y_out[u], sent * 16)
                for j in range(2):
                    act.activation(yo[:, u, 2 * j:2 * j + 2, :].rearrange("p s d -> p (s d)"),
                                   OB[2 * u + j][:, :], ACT.Copy).then_inc(o_ready, 1)

            split_in(0)
            expert(0, 0, 0, 1)
            expert(1, 1, 0, 1)
            with act.Fori(1, E // 2 - 1) as i:
                expert(2 * i, 0, i, i + 1)
                expert(2 * i + 1, 1, i, i + 1)
            expert(E - 2, 0, E // 2 - 1, None)
            expert(E - 1, 1, E // 2 - 1, None, last=True)

            G, Q, REC = bank[0:2], bank[2:4], bank[4:6]
            for n in range(EARLY, RA):
                receptance(n, REC[n % 2])
                if n + 2 < RA:
                    high_xr(n + 2, 1 - n % 2, n % 2, 2)

            def flat(t, c):
                return t[:, c, :, :, :].rearrange("p s k b -> p (s k b)")

            def high_x2(n):
                own_wait()
                act.wait_ge(x2_ready, n + 1)
                wait_past(act, x2_used, n)
                act.activation(flat(x2s, HI), xs[:, pair(n)], ACT.Copy).then_inc(x2_hi, 1)

            def high_x3(n):
                own_wait()
                act.wait_ge(x3_ready, 2 * n + 2)
                wait_past(act, x3_used, n)
                act.activation(flat(x3s, HI), xs[:, pair(n)], ACT.Copy).then_inc(x3_hi, 1)

            def gate2(t, q, s):
                act.wait_ge(g_mm, t + 1)
                for k in range(K):
                    act.activation(g2[:, half(k)], pair_of(G[q])[:, k, s, :], ACT.Sigmoid,
                                   bias=vec[:, V_B2, k:k + 1]).then_inc(g_sig, 1)

            def state2(t, s):
                for k in range(K):
                    act.wait_ge(pre_ready, 2 * t + k + 1)
                    act.activation(h2[:, s, half(k)], pre[:, half(k)], ACT.Tanh).then_inc(h2_ready, 1)

            def state3(t, q, s, n):
                wait_past(act, out_ready, n - 1)
                act.wait_ge(p3_mm, t + 1)
                for k in range(K):
                    a = act.activation(h3[:, 2 * q + s, half(k)], pair_of(Q[q])[:, k, s, :], ACT.Tanh,
                                       bias=vec[:, V_B3, k:k + 1])
                a.then_inc(h3_ready, 1)

            def pair_c(n, q, i, ahead):
                if exists(n - 1):
                    high_x3(n - 1)
                if exists(n):
                    gate2(2 * n, q, 0)
                if exists(n - 2):
                    state3(2 * n - 4, q, 0, n - 2)
                if exists(n):
                    state2(2 * n, 0)
                if ahead and exists(n + RA, start=RA):
                    high_xr(n + RA, 1 - parity(q), parity(q), 2)
                if exists(n - 2):
                    state3(2 * n - 3, q, 1, n - 2)
                if exists(n):
                    gate2(2 * n + 1, q, 1)
                if exists(n + 2):
                    high_x2(n + 2)
                if exists(n):
                    state2(2 * n + 1, 1)
                if ahead and exists(n + RA, start=RA):
                    receptance(n + RA, REC[parity(q)])

            over_pairs(act, pair_c)

        @block.vector
        def _(dve):
            gates = [bank[0:2], bank[2:4], bank[4:6]]
            MISC = bank[6]
            dve.memset(zeros[:, :], 0.0).then_inc(zeros_set, 1)
            dve.memset(h[:, 0, :], 0.0).then_inc(h_ready, K)

            chain = [0]

            def link(ins):
                chain[0] += 1
                ins.then_inc(route_step, 1)
                dve.wait_ge(route_step, chain[0])

            def route():
                dve.wait_ge(id_in, 16)
                link(dve.tensor_single_scalar(id_i[:, :], id_i[:, :], E - 1, ALU.bitwise_and))
                link(dve.tensor_single_scalar(id_i[:, :], id_i[:, :], float(HASH), ALU.mult))
                link(dve.tensor_single_scalar(id_i[:, :], id_i[:, :], E - 1, ALU.bitwise_and))
                link(dve.tensor_copy(ef[:, :], id_i[:, :]))
                dve.wait_ge(consts, 1)
                link(dve.tensor_tensor(onehot[:, :, :], eidx[:, :, :],
                                       ef[:, :].unsqueeze(1).broadcast_to([P, E, T]), ALU.is_equal))
                dve.wait_ge(consts, 2)
                link(dve.tensor_tensor_scan(count[:, :], carry[:, :], onehot[:, :, :].rearrange("p e t -> p (e t)"),
                                            0.0, ALU.mult, ALU.add))
                count3 = count[:, :].rearrange("p (e t) -> p e t", t=T)
                dve.tensor_copy(total[:, :], count3[:, :, T - 1:T].rearrange("p e t -> p (e t)"))\
                   .then_inc(total_ready, 1)

            def place(part):
                count3 = count[:, :].rearrange("p (e t) -> p e t", t=T)
                if part == 0:
                    dve.wait_ge(before_mm, 1)
                    link(dve.tensor_copy(before[:, :], MISC[:, 0:E]))
                    link(dve.tensor_tensor(count3, count3, before[:, :].unsqueeze(2).broadcast_to([P, E, T]),
                                           ALU.add))
                if part == 1:
                    link(dve.tensor_tensor(count3, count3, onehot[:, :, :], ALU.mult))
                if part == 2:
                    link(dve.tensor_reduce(pos[:, :], count3.rearrange("p e t -> p t e"), AX.X, ALU.add))
                if part == 3:
                    link(dve.tensor_single_scalar(keep[:, :], pos[:, :], float(C), ALU.is_le))
                    link(dve.tensor_scalar(slot_f[:, :], ef[:, :], float(C), float(-1 - NSLOT), ALU.mult, ALU.add))
                    link(dve.tensor_tensor(slot_f[:, :], slot_f[:, :], pos[:, :], ALU.add))
                    link(dve.tensor_tensor(slot_f[:, :], slot_f[:, :], keep[:, :], ALU.mult))
                    dve.tensor_scalar(slot_i[:, :], slot_f[:, :], float(NSLOT), None, ALU.add)\
                       .then_inc(slots_ready, 1)

            def low(dst, src, high, done):
                dve.tensor_tensor(dst, src, high.bitcast(F32), ALU.subtract).then_inc(done, 1)

            def low_matrix(m):
                dve.wait_ge(ws_hi, m + 1)
                low(wr[:, m, LO, :, :], wsrc[:, m, :, :], wr[:, m, HI, :, :], ws_lo)

            def low_x(n, q):
                dve.wait_ge(x_hi, n + 1)
                f = [xsp[:, q, c, :, :, :].rearrange("p s k b -> p (s k b)") for c in (HI, LO)]
                low(f[LO], xs[:, pair(n)], f[HI], x_lo)

            route()
            low_x(0, 0)
            place(0)
            for m in range(3):
                low_matrix(m)

            def add_cond(g, n, q):
                if isinstance(n, int) and n == 0:
                    dve.wait_ge(v_ready, g + 1)
                dve.wait_ge(proj_mm[g], n + 1)
                bk = gates[g][q]
                dve.tensor_tensor(bk[:, :], bk[:, :], v2[:, g, :, :, :].rearrange("p k s b -> p (k s b)"),
                                  ALU.add).then_inc(cond_in[g], 1)

            for g in range(3):
                add_cond(g, 0, 0)
            low_x(1, 1)

            def mix(t, u):
                dve.wait_ge(dx_ready, t + 1)
                wait_past(dve, tr_mm, t)
                for k in range(K):
                    a = dve.scalar_tensor_tensor(xk[:, half(k)], dx[:, u, half(k)], vec[:, V_MK, k:k + 1],
                                                 xs[:, bass.ds(t * W + W + k * B, B)], ALU.mult, ALU.add)
                a.then_inc(xk_ready, 1)

            def low_first(j):
                part = [(wkr, wvr)[j][:, 0, c, :, :].rearrange("p a b -> p (a b)") for c in (HI, LO)]
                dve.wait_ge((key_hi, value_hi)[j], 1)
                low(part[LO], wkv[:, 0, j, :], part[HI], w_lo)

            def mix_r(n, p, bufs):
                dve.wait_ge(dx2_ready, n + 1)
                wait_past(dve, xr_lo, n + 1 - bufs)
                xr3, dx3 = (v[p][:, :].rearrange("p (s k b) -> p s k b", s=2, k=K) for v in (xr, dx2))
                x3 = xs[:, pair(n)].rearrange("p (s k b) -> p s k b", s=2, k=K)
                for k in range(K):
                    a = dve.scalar_tensor_tensor(xr3[:, :, k, :], dx3[:, :, k, :], vec[:, V_MR, k:k + 1],
                                                 x3[:, :, k, :], ALU.mult, ALU.add)
                a.then_inc(xr_ready, 1)

            def low_xr(n, src, p):
                dve.wait_ge(xr_hi, n + 1)
                f = [xrs[p][:, c, :, :, :].rearrange("p s k b -> p (s k b)") for c in (HI, LO)]
                low(f[LO], xr[src][:, :], f[HI], xr_lo)

            def spare(t):
                if t < 3:
                    place(t + 1)
                if T - 8 <= t < T - 5:
                    low_matrix(3 + t - (T - 8))
                if t == T - 5:
                    mix_r(0, 0, 1)
                if t == T - 4:
                    low_xr(0, 0, 0)
                if t == T - 3:
                    mix_r(1, 0, 1)
                if t == T - 2:
                    low_first(0)
                    low_xr(1, 0, 0)

            def pair_a(n, q):
                for s in range(2):
                    t = 2 * n + s
                    hp, hn = h[:, s, :], h[:, 1 - s, :]
                    dve.wait_ge(h_ready, 2 * t + 2)
                    dve.wait_ge(r_sig, t + 1)
                    for k in range(K):
                        dve.tensor_tensor(rg[:, k, :], rg[:, k, :], hp[:, half(k)], ALU.mult).then_inc(rh_ready, 1)
                    dve.wait_ge(z_sig, t + 1)
                    dve.scalar_tensor_tensor(wh[:, :], zg[:, :, :].rearrange("p k b -> p (k b)"), 1.0, hp,
                                             ALU.subtract, ALU.mult).then_inc(wh_ready, 1)
                    if exists(t - 1, end=T):
                        mix(t - 1, 1 - s)
                    dve.wait_ge(c_tanh, t + 1)
                    c = hh[:, :, :].rearrange("p k b -> p (k b)")
                    dve.tensor_tensor(c, zg[:, :, :].rearrange("p k b -> p (k b)"), c, ALU.mult).then_inc(ph_ready, 1)
                    dve.wait_ge(wh_ready, t + 1)
                    dve.wait_ge(ph_ready, t + 1)
                    wait_past(dve, x1_ready, t)
                    for k in range(K):
                        dve.tensor_tensor(hn[:, half(k)], hh[:, k, :], wh[:, half(k)], ALU.subtract)\
                           .then_inc(h_ready, 1)
                    if exists(n + 1):
                        if s == 0:
                            add_cond(0, n + 1, 1 - q)
                        else:
                            add_cond(1, n + 1, 1 - q)
                            add_cond(2, n + 1, 1 - q)
                    if s == 0 and exists(n + 2):
                        low_x(n + 2, q)
                    if isinstance(t, int):
                        spare(t)

            for n in range(4):
                pair_a(n, n % 2)
            with dve.Fori(2, NP // 2 - 2) as i:
                pair_a(2 * i, 0)
                pair_a(2 * i + 1, 1)
            for n in range(NP - 4, NP):
                pair_a(n, n % 2)
            t = T - 1
            dve.wait_ge(h_ready, 2 * t + 4)
            dve.tensor_tensor(xs[:, at(t)], xs[:, at(t)], h[:, 0, :], ALU.add).then_inc(x1_ready, 1)
            dve.wait_ge(x1_ready, t + 1)
            dve.wait_ge(xk_ready, t - 1)
            dve.tensor_tensor(dx[:, 1, :], xs[:, at(t - 1)], xs[:, at(t)], ALU.subtract).then_inc(dx_ready, 1)
            mix(t, 1)

            for n in range(2, EARLY):
                mix_r(n, 0, 1)
                low_xr(n, 0, 0)
                if n == 2:
                    low_first(1)
            mix_r(EARLY, 0, 1)

            TT = bank[0:2]

            def low_in(e):
                for k in range(K):
                    dve.wait_ge(ein_hi, e * K + k + 1)
                    low(einr[:, LO, k, :], TT[k][:, :], einr[:, HI, k, :], ein_lo)

            def low_sq(e, f):
                dve.wait_ge(hid_hi, e * FT + f + 1)
                low(hidr[:, LO, f, :], hsq[:, f % 2, :], hidr[:, HI, f, :], hid_lo)

            def expert(e, last=False):
                for f in range(FT):
                    dve.wait_ge(rel_ready, e * FT + f + 1)
                    if f == 0:
                        wait_past(dve, o_mm, e)
                    wait_past(dve, hid_lo, e * FT + f - 1)
                    dve.tensor_tensor(hsq[:, f % 2, :], hrel[:, f % 2, :], hrel[:, f % 2, :], ALU.mult)\
                       .then_inc(sq_ready, 1)
                    if f > 0:
                        low_sq(e, f - 1)
                low_sq(e, FT - 1)
                if not last:
                    low_in(e + 1)

            low_in(0)
            expert(0)
            low_xr(EARLY, 0, 0)
            mix_r(EARLY + 1, 0, 1)
            with dve.Fori(1, E - 1) as e:
                expert(e)
            expert(E - 1, last=True)

            Y = bank[6:8]
            dve.wait_ge(w_lo, 2 * E)
            for n in range(EARLY + 1, RA):
                mix_r(n + 1, (n + 1 + 1) % 2, 2)
                low_xr(n, (n + 1) % 2, n % 2)
            dve.wait_ge(y_out[0], 16 * (E // 2))
            dve.wait_ge(y_out[1], 16 * (E // 2))
            dve.tensor_scalar(leak_t[:, :].rearrange("p (k b) -> p k b", k=K),
                              vec[:, V_AL, :].unsqueeze(2).broadcast_to([P, K, B]), -1.0, 1.0,
                              ALU.mult, ALU.add).then_inc(leak_ready, 1)
            dve.tensor_copy(h2[:, 1, :], xs[:, 0:W]).then_inc(h2_ready, K)
            dve.tensor_copy(h3[:, 3, :], xs[:, 0:W]).then_inc(h3_ready, 1)

            def flat(t, c):
                return t[:, c, :, :, :].rearrange("p s k b -> p (s k b)")

            def gate_y(n, q):
                dve.wait_ge(yT_mm, 2 * n + 2)
                dve.wait_ge(rec_sig, n + 1)
                dve.tensor_tensor(rr_of(n), Y[q][:, :], rr_of(n), ALU.mult).then_inc(ry_ready, 1)

            def low_x2(n):
                dve.wait_ge(x2_hi, n + 1)
                low(flat(x2s, LO), xs[:, pair(n)], flat(x2s, HI), x2_lo)

            def low_x3(n):
                dve.wait_ge(x3_hi, n + 1)
                low(flat(x3s, LO), xs[:, pair(n)], flat(x3s, HI), x3_lo)

            def decay(t, s):
                dve.wait_ge(h2_ready, 2 * t + 2)
                dve.tensor_tensor(hl[:, :], h2[:, 1 - s, :], leak_t[:, :], ALU.mult).then_inc(hl_ready, 1)

            def inner(t):
                for k in range(K):
                    dve.wait_ge(g_sig, 2 * t + k + 1)
                    dve.tensor_tensor(gz[:, half(k)], g2[:, half(k)], xs[:, bass.ds(t * W + W + k * B, B)], ALU.mult)\
                       .then_inc(gz_ready, 1)
                dve.wait_ge(hl_ready, t + 1)
                for k in range(K):
                    dve.wait_ge(gz_ready, 2 * t + k + 1)
                    dve.tensor_tensor(pre[:, half(k)], gz[:, half(k)], hl[:, half(k)], ALU.add).then_inc(pre_ready, 1)

            def add_h2(t, s):
                dve.wait_ge(h2_ready, 2 * t + 4)
                dve.tensor_tensor(xs[:, at(t)], xs[:, at(t)], h2[:, s, :], ALU.add).then_inc(x3_ready, 1)

            def pair_c(n, q, i, ahead):
                if exists(n - 1):
                    low_x3(n - 1)
                if exists(n):
                    inner(2 * n)
                if exists(n + 2):
                    gate_y(n + 2, q)
                if isinstance(n, int) and n + 2 == 0:
                    dve.wait_ge(ry_ready, 1)
                    dve.tensor_tensor(xs[:, pair(0)], xs[:, pair(0)], rr_of(0), ALU.add).then_inc(x2_ready, 1)
                if exists(n):
                    add_h2(2 * n, 0)
                    decay(2 * n + 1, 1)
                if ahead and exists(n + RA, start=RA):
                    low_xr(n + RA, 1 - parity(q), parity(q))
                if ahead and exists(n + RA + 1, start=RA + 1):
                    mix_r(n + RA + 1, parity(q), 2)
                if exists(n):
                    inner(2 * n + 1)
                if exists(n + 2):
                    low_x2(n + 2)
                if exists(n):
                    add_h2(2 * n + 1, 1)
                if exists(n + 1):
                    decay(2 * n + 2, 0)

            over_pairs(dve, pair_c)
            n = NP - 1
            dve.wait_ge(h3_ready, T + 1)
            dve.wait_ge(out_ready, n)
            dve.tensor_tensor(xs[:, pair(n)], xs[:, pair(n)], h3[:, 2:4, :].rearrange("p s w -> p (s w)"),
                              ALU.add).then_inc(out_ready, 1)

        @block.gpsimd
        def _(pool):
            def own_wait():
                pool.wait_ge(zeros_set, 1)

            pool.iota(eidx[:, :, :], [[1, E], [0, T]], base=0, channel_multiplier=0,
                      allow_small_or_imprecise_dtypes=True).then_inc(consts, 1)
            pool.memset(carry[:, :], 1.0).then_inc(const_step, 1)
            pool.memset(lower[:, :], 1.0).then_inc(const_step, 1)
            pool.memset(ident[:, :], 0.0).then_inc(const_step, 1)
            pool.wait_ge(const_step, 3)
            carry3 = carry[:, :].rearrange("p (e t) -> p e t", t=T)
            pool.affine_select(carry3, carry3, pattern=[[0, E], [1, T]], compare_op=ALU.is_gt, fill=0.0,
                               base=0, channel_multiplier=0).then_inc(consts, 1)
            pool.affine_select(lower[:, :], lower[:, :], pattern=[[1, P]], compare_op=ALU.is_gt, fill=0.0,
                               base=0, channel_multiplier=-1).then_inc(consts, 1)
            pool.affine_select(ident[:, :], ident[:, :], pattern=[[-1, P]], compare_op=ALU.not_equal, fill=1.0,
                               base=0, channel_multiplier=1).then_inc(consts, 1)
            last_slot, zero_row = pool.to_reg(NSLOT - 1), pool.to_reg(NSLOT)

            def step_a(t, u):
                pool.wait_ge(h_ready, 2 * t + 4)
                pool.sem_inc(pool_paced, 1)
                pool.tensor_tensor(xs[:, at(t)], xs[:, at(t)], h[:, 1 - u, :], ALU.add).then_inc(x1_ready, 1)
                pool.wait_ge(x1_ready, t + 1)
                wait_past(pool, xk_ready, t - 1)
                pool.sem_inc(pool_paced, 1)
                pool.tensor_tensor(dx[:, u, :], xs[:, at(t - 1)], xs[:, at(t)], ALU.subtract).then_inc(dx_ready, 1)

            def scatter(t, u, sent):
                wait_past(pool, scat[u], sent * 16)
                pool.tensor_copy(idx[:, u:u + 1], slot_i[:, bass.ds(t, 1)]).then_inc(idx_ready, 1)
                pool.wait_ge(idx_ready, t + 1)
                pool.wait_ge(row_ready, t + 1)
                pool.sem_inc(pool_paced, 1)
                pool.indirect_dma_start(rows, bass.IndirectOffsetOnAxis(idx[:, u:u + 1], axis=0), row[:, u, :], None,
                                        bounds_check=last_slot, oob_is_err=False).then_inc(scat[u], 16)

            def deltas(n, p, bufs):
                wait_past(pool, xr_ready, n + 1 - bufs)
                own_wait()
                pool.tensor_tensor(dx2[p][:, :], xs[:, pair(n, before=1)], xs[:, pair(n)], ALU.subtract)\
                    .then_inc(dx2_ready, 1)

            def pair_a(n, q, i):
                for s in range(2):
                    t = 2 * n + s
                    if exists(t, end=T - 1):
                        step_a(t, s)
                    if isinstance(t, int) and t < 3:
                        continue
                    if isinstance(t, int) and t == 3:
                        pool.wait_ge(slots_ready, 1)
                        pool.wait_ge(zfill, 16 * (ZPARTS + 1))
                        scatter(0, 0, 0)
                        scatter(1, 1, 0)
                    scatter(t - 1, (2 * q + s - 1) % 4, i - 1 if q == s == 0 else i)
                    if isinstance(t, int) and t == T - 8:
                        deltas(0, 0, 1)
                    if isinstance(t, int) and t == T - 4:
                        deltas(1, 0, 1)
                    if isinstance(t, int) and t == T - 2:
                        deltas(2, 0, 1)

            for n in range(4):
                pair_a(n, n % 2, n // 2)
            with pool.Fori(2, NP // 2 - 2) as i:
                pair_a(2 * i, 0, i)
                pair_a(2 * i + 1, 1, i)
            for n in range(NP - 4, NP):
                pair_a(n, n % 2, n // 2)
            scatter(T - 1, 3, T // 4 - 1)

            for n in range(3, EARLY + 2):
                deltas(n, 0, 1)

            def split_weights(e, u, n):
                pool.wait_ge(kv_in[u], (n + 1) * 32)
                wait_past(pool, o_mm, e - 1)
                key, value = ([wide[:, u, c, :, :].rearrange("p a b -> p (a b)") for c in (HI, LO)]
                              for wide in (wkr, wvr))
                pool.wait_ge(key_hi, e + 1)
                pool.tensor_tensor(key[LO], wkv[:, u, 0, :], key[HI].bitcast(F32), ALU.subtract).then_inc(w_lo, 1)
                pool.sem_inc(pool_paced, 1)
                pool.tensor_copy(value[HI], wkv[:, u, 1, :]).then_inc(value_hi, 1)
                pool.wait_ge(value_hi, e + 1)
                pool.tensor_tensor(value[LO], wkv[:, u, 1, :], value[HI].bitcast(F32), ALU.subtract).then_inc(w_lo, 1)

            pool.wait_ge(w_lo, 2)
            split_weights(1, 1, 0)
            with pool.Fori(1, E // 2) as i:
                split_weights(2 * i, 0, i)
                split_weights(2 * i + 1, 1, i)

            def gather(n, q, s, done):
                t, u = 2 * n + s, 2 * q + s
                wait_past(pool, gath[u], done * 16)
                wait_past(pool, yT_mm, t - 3)
                pool.tensor_copy(idx[:, u:u + 1], slot_i[:, bass.ds(t, 1)]).then_inc(idy_ready, 1)
                pool.wait_ge(idy_ready, t + 1)
                pool.sem_inc(pool_paced, 1)
                pool.indirect_dma_start(yrow[:, u, :], None, yrows, bass.IndirectOffsetOnAxis(idx[:, u:u + 1], axis=0),
                                        bounds_check=zero_row, oob_is_err=False).then_inc(gath[u], 16)

            def add_y(n, q):
                pool.wait_ge(ry_ready, n + 1)
                if exists(n + 1):
                    pool.wait_ge(dx2_ready, n + 2)
                pool.sem_inc(pool_paced, 1)
                pool.tensor_tensor(xs[:, pair(n)], xs[:, pair(n)], rr_of(n), ALU.add).then_inc(x2_ready, 1)

            def add_h3(n, q):
                pool.wait_ge(h3_ready, 2 * n + 3)
                pool.sem_inc(pool_paced, 1)
                pool.tensor_tensor(xs[:, pair(n)], xs[:, pair(n)],
                                   h3[:, 2 * q:2 * q + 2, :].rearrange("p s w -> p (s w)"), ALU.add)\
                    .then_inc(out_ready, 1)

            def pair_c(n, q, i, ahead):
                if ahead and exists(n + RA + 1, start=RA + 1):
                    deltas(n + RA + 1, parity(q), 2)
                if exists(n + 2, start=1):
                    add_y(n + 2, q)
                if exists(n + 4):
                    for s in range(2):
                        gather(n + 4, q, s, i + 2)
                if exists(n - 2, end=NP - 1):
                    add_h3(n - 2, q)

            pool.wait_ge(w_lo, 2 * E)
            for n in range(EARLY + 2, RA + 1):
                deltas(n, (n + 1) % 2, 2)
            pool.wait_ge(y_out[0], 16 * (E // 2))
            pool.wait_ge(y_out[1], 16 * (E // 2))
            over_pairs(pool, pair_c)


def _halves(a):
    return a.reshape(K, P, -1).transpose(1, 0, 2)


def kernel(x, cond_1024, itok_BxS_2_50255, L0_cond_W_z, L0_cond_U_z, L0_cond_C_z, L0_cond_b_z, L0_cond_W_r,
           L0_cond_U_r, L0_cond_C_r, L0_cond_b_r, L0_cond_W, L0_cond_U, L0_cond_C, L0_cond_b,
           L1_cond_time_maa_k, L1_cond_time_maa_r, L1_cond_w_recept, L1_cond_w_key, L1_cond_w_value,
           L2_cond_W, L2_cond_b, L2_cond_alpha, L3_cond_Wx, L3_cond_Wh, L3_cond_b):
    import concourse.bacc as bacc
    from concourse.bass_utils import run_bass_kernel_spmd

    a = np.asarray
    l2 = a(L2_cond_W).T
    cmats = [L0_cond_C_r, L0_cond_C_z, L0_cond_C]
    mats = [L0_cond_U_r, L0_cond_U_z, L0_cond_U, l2[:D], L3_cond_Wh]
    smats = [L0_cond_W_r, L0_cond_W_z, L0_cond_W, a(L1_cond_w_recept).T, l2[D:], L3_cond_Wx]
    vecs = [L0_cond_b_z, L0_cond_b_r, L0_cond_b, L1_cond_time_maa_k, L1_cond_time_maa_r, L2_cond_b, L2_cond_alpha,
            L3_cond_b]
    laid = {
        "x": a(x).reshape(B, T, K, P).transpose(3, 1, 2, 0).reshape(P, T * W),
        "cond": a(cond_1024).reshape(B, K, P).transpose(2, 1, 0).reshape(P, W),
        "ids": a(itok_BxS_2_50255),
        "cmats": np.stack([_halves(a(m)) for m in cmats], 1),
        "mats": np.stack([_halves(a(m)) for m in mats], 1),
        "smats": np.stack([_halves(a(m)) for m in smats], 1),
        "vecs": np.stack([a(v).reshape(K, P).T for v in vecs], 1),
        "w_key": a(L1_cond_w_key).reshape(E, K, P, F).transpose(2, 0, 1, 3).reshape(P, E * K * F),
        "w_value": a(L1_cond_w_value).reshape(E, FT, P, D).transpose(2, 0, 1, 3).reshape(P, E * FT * D),
    }
    laid = {n: np.ascontiguousarray(v) for n, v in laid.items()}

    nc = bacc.Bacc("TRN2", target_bir_lowering=False, num_devices=1)
    args = [nc.dram_tensor(n, v.shape, mybir.dt.from_np(v.dtype), kind="ExternalInput").ap() for n, v in laid.items()]
    out = nc.dram_tensor("out", (P, T * W), F32, kind="ExternalOutput").ap()
    rows = nc.dram_tensor("rows", (NSLOT, D), F32, kind="Internal").ap()
    yrows = nc.dram_tensor("yrows", (NSLOT + 1, D), F32, kind="Internal").ap()
    build(nc, *args, out, rows, yrows)
    r = run_bass_kernel_spmd(nc, [laid], core_ids=[0])
    got = r.results[0]["out"]
    return got.reshape(P, T, K, B).transpose(3, 1, 2, 0).reshape(B, T, D)
```
